# Optimizing a Trainium2 kernel written in Bass

```python
import numpy as np
import jax
import jax.numpy as jnp

def _softmax(x, axis=-1):
    return jax.nn.softmax(x, axis=axis)

def _gelu(x):
    return jax.nn.gelu(x, approximate=True)

def _silu(x):
    return jax.nn.silu(x)

def _sigmoid(x):
    return jax.nn.sigmoid(x)

def _layernorm(x, axis=-1, eps=1e-05):
    m = jnp.mean(x, axis=axis, keepdims=True)
    v = jnp.var(x, axis=axis, keepdims=True)
    return (x - m) / jnp.sqrt(v + eps)

def _scatter_add(tgt, idx, src, axis=0):
    return tgt.at[idx].add(src)

def _segment_sum(src, seg, n):
    return jax.ops.segment_sum(src, seg, n)
kernel_name = 'mk_adj_ffn_d1_adj_r2_beff75'

def setup_inputs(seed: int=0):
    np.random.seed(seed)
    _w = jnp.asarray

    def _rec_inputs():
        import jax
        import jax.numpy as jnp
        _gk = jax.random.key(seed)
        x = -0.0002928 + 1 * jax.random.normal(jax.random.fold_in(_gk, 1), (4096, 256), jnp.float32)
        _a = jax.random.bernoulli(jax.random.fold_in(_gk, 2), 0.000488281, (4096, 4096))
        _a = jnp.logical_or(_a, jnp.swapaxes(_a, -1, -2))
        _a = jnp.logical_or(_a, jnp.eye(4096, dtype=bool))
        _af = _a.astype(jnp.float32)
        _af = _af * jax.random.uniform(jax.random.fold_in(_gk, 3), (4096, 4096), jnp.float32, 0.05, 5.41998)
        adj = _af
        return (x, adj)
    x, adj = _rec_inputs()

    def _L0_gnn_setup():
        import jax, jax.numpy as jnp
        import numpy as np
        N = 4096
        D = 256
        EPS = 1e-12
        key = jax.random.key(seed)
        k1, k2 = jax.random.split(key)
        cur = jax.random.normal(k1, (N, D), dtype=jnp.float32)
        incidence_m = jax.random.normal(k2, (N, N), dtype=jnp.float32)
        return {'cur': cur, 'incidence_m': incidence_m}
    _L0_gnn_all = _L0_gnn_setup()
    _L0_gnn_in = {k: v for k, v in _L0_gnn_all.items() if k in ()}
    del _L0_gnn_all

    def _L0_ffn_setup():
        import jax, jax.numpy as jnp
        import numpy as np
        MAX_THRESHOLD = 0.25
        B, S, D, E = (8, 2048, 256, 8)
        key = jax.random.key(seed)
        ks = jax.random.split(key, 5)
        scale = 1.0 / np.sqrt(D)
        return {'inputs': jax.random.normal(ks[0], (B, S, D), dtype=jnp.float32), 'W_gate': jax.random.normal(ks[1], (D, E), dtype=jnp.float32) * scale, 'b_gate': jnp.zeros((E,), dtype=jnp.float32), 'W_thr': jax.random.normal(ks[2], (D, 1), dtype=jnp.float32) * scale, 'b_thr': jnp.zeros((1,), dtype=jnp.float32), 'W_exp': jax.random.normal(ks[3], (E, D, D), dtype=jnp.float32) * scale, 'b_exp': jnp.zeros((E, D), dtype=jnp.float32)}
    _L0_ffn_all = _L0_ffn_setup()
    _L0_ffn_in = {k: v for k, v in _L0_ffn_all.items() if k in ('W_gate', 'b_gate', 'W_thr', 'b_thr', 'W_exp', 'b_exp')}
    del _L0_ffn_all
    return {'x': x, 'adj': adj, 'L0_ffn_W_gate': _L0_ffn_in['W_gate'], 'L0_ffn_b_gate': _L0_ffn_in['b_gate'], 'L0_ffn_W_thr': _L0_ffn_in['W_thr'], 'L0_ffn_b_thr': _L0_ffn_in['b_thr'], 'L0_ffn_W_exp': _L0_ffn_in['W_exp'], 'L0_ffn_b_exp': _L0_ffn_in['b_exp']}

def reference(x, adj, L0_ffn_W_gate, L0_ffn_b_gate, L0_ffn_W_thr, L0_ffn_b_thr, L0_ffn_W_exp, L0_ffn_b_exp):
    import jax
    import jax.numpy as jnp

    def _L0_gnn_ref(cur, incidence_m):
        import jax, jax.numpy as jnp
        import numpy as np
        N = 4096
        D = 256
        EPS = 1e-12
        mask = incidence_m > 0
        head = jax.lax.stop_gradient(mask.astype(incidence_m.dtype))
        head = head / jnp.maximum(jnp.sqrt(jnp.sum(head * head, axis=-1, keepdims=True)), EPS)
        inc = incidence_m + head
        edge_fea = inc @ cur
        edge_degree = jnp.sum(inc, axis=-1, keepdims=True)
        return edge_fea / edge_degree

    def _L0_ffn_ref(inputs, W_gate, b_gate, W_thr, b_thr, W_exp, b_exp):
        import jax, jax.numpy as jnp
        import numpy as np
        MAX_THRESHOLD = 0.25
        B, S, D, E = (8, 2048, 256, 8)
        d = inputs.shape[-1]
        x = inputs.reshape(-1, d)
        gate_logits = jax.nn.softmax(x @ W_gate + b_gate, axis=-1)
        thresholds = jax.nn.sigmoid(x @ W_thr + b_thr) * MAX_THRESHOLD
        adapted = gate_logits - thresholds
        selected = (adapted >= 0).astype(x.dtype)
        weights = adapted * selected
        wsum = jnp.sum(weights, axis=-1, keepdims=True)
        wsum = jnp.where(wsum == 0, jnp.ones_like(wsum), wsum)
        weights = weights / wsum
        ex_out = jnp.einsum('td,edf->etf', x, W_exp) + b_exp[:, None, :]
        results = jnp.einsum('etf,te->tf', ex_out, weights)
        return results.reshape(inputs.shape[:-1] + (results.shape[-1],))
    x = x + _L0_gnn_ref(_layernorm(x, axis=-1), adj)
    x = x + _L0_ffn_ref(_layernorm(x, axis=-1)[None], L0_ffn_W_gate, L0_ffn_b_gate, L0_ffn_W_thr, L0_ffn_b_thr, L0_ffn_W_exp, L0_ffn_b_exp)[0]
    return x

_drawn_inputs = setup_inputs


def setup_inputs(seed=0):
    import zlib

    import numpy as np

    out = dict(_drawn_inputs(seed))
    spreads = {'L0_ffn_b_gate': (0.0, 0.1), 'L0_ffn_b_exp': (0.0, 0.1)}
    factors = {}
    for name, (base, spread) in spreads.items():
        noise = np.random.default_rng([zlib.crc32(name.encode()), seed]).standard_normal(out[name].shape)
        drawn = base * np.exp(spread * noise) if base else spread * noise
        out[name] = jnp.asarray(drawn.astype(out[name].dtype))
    for name, factor in factors.items():
        out[name] = (out[name] * factor).astype(out[name].dtype)
    return out
```

```python
from contextlib import ExitStack

import concourse.bass as bass
from concourse import mybir

F32 = mybir.dt.float32
F32R = mybir.dt.float32r
BF16 = mybir.dt.bfloat16
ALU = mybir.AluOpType
ACT = mybir.ActivationFunctionType
AX = mybir.AxisListType

P = 128
LN_EPS = 1e-5
NORM_EPS = 1e-12
MAX_THRESHOLD = 0.25


def program(nc, x, adj, w_gate, b_gate, w_thr, b_thr, w_exp, b_exp, out):
    N, D = x.shape
    E = w_exp.shape[0]
    DH = D // P
    R = 4
    ROWS = R * P
    G = N // ROWS
    J = N // P
    CB = 4
    C = J // CB
    CW = CB * P
    NE = E + 1
    NEP = E + 2
    XC = 8
    XB = J // XC
    TP = 3
    WC = 4
    WE = DH * E // WC
    HL = 4
    AHEAD = 2
    PAIR = 2
    ITEMS = E // PAIR + 1
    BLOCK_SUMS = E + 1
    COUNT_STEPS = 2
    GATE_STEPS = 15
    SMALL_LOADS = 2 * R + 3
    BACK_AT = (1, 5)
    STAT_AT = 8
    NORMAL_AT = 10
    TURN_AT = (12, 15)
    GATE_AT = 18
    WEIGHT_AT = 25
    COUNT_AT = 6
    WEIGHT_SPLITS = (8, 9, 22, 24)
    EARLY = 2

    adj_rows = adj.rearrange("(g p r) c -> g p r c", p=P, r=R)
    x_rows = x.rearrange("(g p r) d -> g p r d", p=P, r=R)
    out_rows = out.rearrange("(g p r) d -> g p r d", p=P, r=R)
    x_blocks = x.rearrange("(k b p) d -> k p b d", p=P, b=XB)
    w_rows = w_exp.rearrange("e (h p) f -> h p e f", p=P)

    with ExitStack() as ctx:
        def sb(name, shape, dt=F32):
            return ctx.enter_context(nc.sbuf_tensor(name, shape, dt))

        def ps(name, shape):
            return ctx.enter_context(nc.psum_tensor(name, shape, F32))

        def sem(name):
            return ctx.enter_context(nc.semaphore(name))

        inc = sb("inc", [P, R, N])
        xn_hi = sb("xn_hi", [P, J, D], F32R)
        xn_lo = sb("xn_lo", [P, J, D], F32R)
        w_hi = sb("w_hi", [P, DH, E * D], F32R)
        w_lo = sb("w_lo", [P, DH, E * D], F32R)
        stage = sb("stage", [P, 2, XB * D])
        t_hi = sb("t_hi", [P, HL, ROWS], F32R)
        t_lo = sb("t_lo", [P, HL, ROWS], F32R)
        x_res = sb("x_res", [P, R, D])
        x1 = sb("x1", [P, R, D])
        x2_hi = sb("x2_hi", [P, DH, ROWS], F32R)
        x2_lo = sb("x2_lo", [P, DH, ROWS], F32R)
        signs = sb("signs", [P, 2, CW], BF16)
        ident = sb("ident", [P, P])
        minus_half = sb("minus_half", [P, XB])
        sign_bias = sb("sign_bias", [P, 1])
        half = sb("half", [P, R])
        sign_sum = sb("sign_sum", [P, R, C])
        sign_row = sb("sign_row", [P, R])
        count = sb("count", [P, R])
        root = sb("root", [P, R])
        norm = sb("norm", [P, R])
        degree_part = sb("degree_part", [P, R, C])
        degree = sb("degree", [P, R])
        inv_degree = sb("inv_degree", [P, R])
        stats0 = sb("stats0", [P, XB, 6])
        parts0 = sb("parts0", [P, 3, XB])
        mean0 = sb("mean0", [P, XB])
        var0 = sb("var0", [P, XB])
        rstd0 = sb("rstd0", [P, XB])
        stats = sb("stats", [P, R, 6])
        parts = sb("parts", [P, 3, R])
        mean = sb("mean", [P, R])
        var = sb("var", [P, R])
        rstd = sb("rstd", [P, R])
        gate_raw = sb("gate_raw", [P, DH, NEP])
        gate_hi = sb("gate_hi", [P, DH, NEP], F32R)
        gate_lo = sb("gate_lo", [P, DH, NEP], F32R)
        gate_bias = sb("gate_bias", [P, R, NE])
        bias_sb = sb("bias_sb", [E, D])
        logits = sb("logits", [P, R, NE])
        top = sb("top", [P, R])
        shifted = sb("shifted", [P, R, NE])
        expd = sb("expd", [P, R, NE])
        total = sb("total", [P, R])
        inv_total = sb("inv_total", [P, R])
        thr_den = sb("thr_den", [P, R])
        thr = sb("thr", [P, R])
        adapted = sb("adapted", [P, R, E])
        weight = sb("weight", [P, R, E])
        wsum = sb("wsum", [P, R])
        wsum1 = sb("wsum1", [P, R])
        inv_wsum = sb("inv_wsum", [P, R])
        weight_n = sb("weight_n", [P, R, E])

        agg_t = stage[:, 0, :]
        xn2 = stage[:, 1, :]
        weight_t = stage[0:E, 1, 0:ROWS]

        agg = [ps(f"agg{h}", [P, ROWS]) for h in range(DH)]
        tp = [ps(f"tp{k}", [P, ROWS]) for k in range(TP)]
        ffn = [ps(f"ffn{k}", [P, PAIR * D]) for k in range(2)]
        misc = ps("misc", [P, 512])
        gate_out = misc[:, 0:R * NEP].rearrange("p (r e) -> p r e", r=R)

        stage_landed = [sem(f"stage_landed{k}") for k in range(2)]
        adj_landed = [sem(f"adj_landed{c}") for c in range(C)]
        x_res_landed = sem("x_res_landed")
        small_landed = sem("small_landed")
        stored = sem("stored")
        zeroed = sem("zeroed")
        consts_ready = sem("consts_ready")
        var0_ready = sem("var0_ready")
        rstd0_ready = sem("rstd0_ready")
        stats0_ready = sem("stats0_ready")
        merge0_step = sem("merge0_step")
        xn_ready = sem("xn_ready")
        xn_hi_ready = sem("xn_hi_ready")
        xn_lo_ready = sem("xn_lo_ready")
        w_hi_ready = sem("w_hi_ready")
        w_lo_ready = sem("w_lo_ready")
        counted = sem("counted")
        count_step = sem("count_step")
        root_ready = sem("root_ready")
        norm_ready = sem("norm_ready")
        scaled = sem("scaled")
        inc_ready = sem("inc_ready")
        transposed = sem("transposed")
        hi_ready = sem("hi_ready")
        lo_ready = sem("lo_ready")
        multiplied = sem("multiplied")
        degree_step = sem("degree_step")
        agg_out = sem("agg_out")
        agg_back = sem("agg_back")
        x1_ready = sem("x1_ready")
        stats_ready = sem("stats_ready")
        merge_step = sem("merge_step")
        var_ready = sem("var_ready")
        rstd_ready = sem("rstd_ready")
        xn2_ready = sem("xn2_ready")
        x2_turned = sem("x2_turned")
        x2_hi_ready = sem("x2_hi_ready")
        x2_lo_ready = sem("x2_lo_ready")
        gate_ready = sem("gate_ready")
        gate_step = sem("gate_step")
        exp_ready = sem("exp_ready")
        weight_turned = sem("weight_turned")
        weight_t_ready = sem("weight_t_ready")
        experts_ready = sem("experts_ready")
        combined = sem("combined")

        def after(g, per, n):
            return g * per + n

        def x_part(t, k):
            return t[:, k * XB:(k + 1) * XB, :]

        def w_part(t, k):
            h, e = divmod(k * WE, E)
            return t[:, h, e * D:(e + WE) * D]

        def passes(fn, engine):
            for first in range(2):
                fn(first, first)
            with engine.Fori(2, G - 1) as g:
                fn(g, None)
            fn(G - 1, G - 1)

        def has_experts(known):
            return known is None or known >= 2

        def chunk(c):
            return slice(c * CW, (c + 1) * CW)

        block = ctx.enter_context(nc.Block())

        @block.sync
        def _(sp):
            def load_adj(g, c):
                sp.dma_start(inc[:, :, chunk(c)], adj_rows[g, :, :, chunk(c)]).then_inc(adj_landed[c], 16)

            def load_x_res(g):
                sp.dma_start(x_res[:, :, :], x_rows[g]).then_inc(x_res_landed, 16)

            def store(g, half):
                sp.wait_ge(combined, after(g, R * BLOCK_SUMS, (2 * half + 2) * BLOCK_SUMS))
                sp.dma_start(out_rows[g, :, 2 * half:2 * half + 2, :],
                             x1[:, 2 * half:2 * half + 2, :]).then_inc(stored, 16)

            for k in range(XC):
                if k >= 2:
                    sp.wait_ge(xn_hi_ready, k - 1)
                    sp.wait_ge(xn_lo_ready, k - 1)
                sp.dma_start(stage[:, k % 2, :].rearrange("p (b d) -> p b d", d=D), x_blocks[k]
                             ).then_inc(stage_landed[k % 2], 16)
            for c in range(C):
                load_adj(0, c)
            load_x_res(0)
            for e in range(R):
                sp.dma_start(gate_bias[:, e, 0:E], b_gate.rearrange("(a e) -> a e", a=1).to_broadcast([P, E])
                             ).then_inc(small_landed, 16)
                sp.dma_start(gate_bias[:, e, E:NE], b_thr.rearrange("(a e) -> a e", a=1).to_broadcast([P, 1])
                             ).then_inc(small_landed, 16)
            sp.dma_start(bias_sb[:, :], b_exp).then_inc(small_landed, 16)
            sp.wait_ge(zeroed, 1)
            with nc.allow_non_contiguous_dma(reason="gate weights of a few bytes a row"):
                sp.dma_start(gate_raw[:, :, 0:E], w_gate.rearrange("(h p) e -> p h e", p=P)
                             ).then_inc(small_landed, 16)
                sp.dma_start(gate_raw[:, :, E:NE], w_thr.rearrange("(h p) e -> p h e", p=P)
                             ).then_inc(small_landed, 16)

            def load_weights(k):
                if k < 2:
                    sp.wait_ge(xn_hi_ready, XC - 1 + k)
                    sp.wait_ge(xn_lo_ready, XC - 1 + k)
                else:
                    sp.wait_ge(w_hi_ready, k - 1)
                    sp.wait_ge(w_lo_ready, k - 1)
                h, e = divmod(k * WE, E)
                sp.dma_start(stage[:, k % 2, :].rearrange("p (e f) -> p e f", e=WE),
                             w_rows[h, :, e:e + WE, :]).then_inc(stage_landed[k % 2], 16)

            for k in range(2):
                load_weights(k)

            def group(g, known):
                if has_experts(known):
                    store(g - 2, 0)
                    store(g - 2, 1)
                for c in range(C):
                    if known != G - 1:
                        sp.wait_ge(transposed, after(g, J, (c + 1) * CB))
                        load_adj(g + 1, c)
                    if c == C // 2 and known == 0:
                        for k in range(2, WC):
                            load_weights(k)
                    if c == C // 2 and known != 0:
                        sp.wait_ge(x1_ready, after(g - 1, R, R))
                        load_x_res(g)

            passes(group, sp)
            for g in (G - 2, G - 1):
                for half in range(2):
                    store(g, half)
            sp.wait_ge(stored, 16 * 2 * G)

        @block.gpsimd
        def _(pool):
            nc.gpsimd.memset(gate_raw[:, :, :], 0.0).then_inc(zeroed, 1)
            nc.gpsimd.memset(ident[:, :], 0.0).then_inc(zeroed, 1)
            nc.gpsimd.memset(minus_half[:, :], -0.5).then_inc(consts_ready, 1)
            nc.gpsimd.memset(half[:, :], 0.5).then_inc(consts_ready, 1)
            nc.gpsimd.memset(sign_bias[:, :], -2.0 ** -120).then_inc(consts_ready, 1)
            pool.wait_ge(zeroed, 2)
            nc.gpsimd.affine_select(out=ident[:, :], in_=ident[:, :], compare_op=ALU.not_equal, fill=1.0,
                                    base=0, pattern=[[-1, P]], channel_multiplier=1).then_inc(consts_ready, 1)
            pool.wait_ge(consts_ready, 4)
            for k in range(XC):
                pool.wait_ge(var0_ready, k + 1)
                nc.gpsimd.tensor_tensor(rstd0[:, :], var0[:, :], minus_half[:, 0:XB], ALU.pow
                                        ).then_inc(rstd0_ready, 1)

            def scale_rows(g, c, r):
                if c == 0 and r == 0:
                    pool.wait_ge(norm_ready, g + 1)
                    nc.gpsimd.tensor_tensor(inc[:, r, chunk(c)], inc[:, r, chunk(c)],
                                            norm[:, r:r + 1].to_broadcast([P, CW]), ALU.mult).then_inc(scaled, 1)
                else:
                    nc.gpsimd.tensor_scalar(inc[:, r, chunk(c)], inc[:, r, chunk(c)], norm[:, r:r + 1], 1.0,
                                            ALU.mult, ALU.mult).then_inc(scaled, 1)

            def group(g, known):
                pool.wait_ge(count_step, after(g, COUNT_STEPS, 2))
                nc.gpsimd.tensor_tensor(root[:, :], count[:, :], half[:, :], ALU.pow).then_inc(root_ready, 1)
                for c in range(C):
                    for r in range(R):
                        scale_rows(g, c, r)
                    if c == C // 2 and known != 0:
                        inverse_deviation(g - 1)

            def inverse_deviation(g):
                pool.wait_ge(var_ready, g + 1)
                nc.gpsimd.tensor_tensor(rstd[:, :], var[:, :], minus_half[:, 0:R], ALU.pow
                                        ).then_inc(rstd_ready, 1)

            passes(group, pool)
            inverse_deviation(G - 1)

        @block.scalar
        def _(act):
            def count_rows(g, c, r):
                if r == 0:
                    act.wait_ge(adj_landed[c], after(g, 16, 16))
                if r % 2 == 0 and not (isinstance(g, int) and g * C + c + r == 0):
                    act.wait_ge(counted, after(g, R * C, c * R + r))
                nc.scalar.activation(signs[:, r % 2, :], inc[:, r, chunk(c)], ACT.Sign,
                                     bias=sign_bias[:, 0:1], scale=2.0 ** 100,
                                     accum_out=sign_sum[:, r, c:c + 1]).then_inc(counted, 1)

            def high(g, known, j):
                act.wait_ge(transposed, after(g, J, j + 1))
                if j >= HL:
                    act.wait_ge(multiplied, after(g, J, j - HL + 1))
                elif known != 0:
                    act.wait_ge(multiplied, after(g, J, j - HL + 1))
                nc.scalar.activation(t_hi[:, j % HL, :], tp[j % TP][:, :], ACT.Copy).then_inc(hi_ready, 1)

            def split_weights(k):
                act.wait_ge(stage_landed[k % 2], 16 * (XC // 2 + k // 2 + 1))
                nc.scalar.activation(w_part(w_hi, k), stage[:, k % 2, :], ACT.Copy).then_inc(w_hi_ready, 1)

            def post(g, j):
                for h in range(DH):
                    if j == TURN_AT[h] + 1:
                        act.wait_ge(x2_turned, after(g, DH, h + 1))
                        nc.scalar.activation(x2_hi[:, h, :], misc[:, :], ACT.Copy).then_inc(x2_hi_ready, 1)
                if j == GATE_AT + 2:
                    act.wait_ge(gate_step, after(g, GATE_STEPS, 4))
                    nc.scalar.activation(expd[:, :, :], shifted[:, :, :], ACT.Exp).then_inc(exp_ready, 1)
                if j == WEIGHT_AT + 1:
                    act.wait_ge(weight_turned, g + 1)
                    nc.scalar.activation(weight_t, misc[0:E, :], ACT.Copy).then_inc(weight_t_ready, 1)

            act.wait_ge(consts_ready, 4)
            for k in range(XC):
                act.wait_ge(xn_ready, k + 1)
                nc.scalar.activation(x_part(xn_hi, k), stage[:, k % 2, :].rearrange("p (b d) -> p b d", d=D),
                                     ACT.Copy).then_inc(xn_hi_ready, 1)
            for c in range(C):
                for r in range(R):
                    count_rows(0, c, r)

            def group(g, known):
                for j in range(AHEAD):
                    high(g, known, j)
                for j in range(J):
                    if j + AHEAD < J:
                        high(g, known, j + AHEAD)
                    n = j - COUNT_AT
                    if 0 <= n < (C - 2) * R and known != G - 1:
                        if n == 0:
                            act.wait_ge(count_step, after(g, COUNT_STEPS, 1))
                        count_rows(g + 1, n // R, n % R)
                    if known != 0:
                        post(g - 1, j)
                    if known == 0 and j in WEIGHT_SPLITS:
                        split_weights(WEIGHT_SPLITS.index(j))
                if known == 0:
                    act.wait_ge(small_landed, 16 * SMALL_LOADS)
                    nc.scalar.activation(gate_hi[:, :, :], gate_raw[:, :, :], ACT.Copy).then_inc(w_hi_ready, 1)
                if known != G - 1:
                    for r in range(R):
                        count_rows(g + 1, C - 2, r)
                act.wait_ge(multiplied, after(g, J, J))
                for h in range(DH):
                    if known != 0 and h == 0:
                        act.wait_ge(agg_back, after(g - 1, 2, 2))
                    nc.scalar.activation(agg_t[:, h * ROWS:(h + 1) * ROWS], agg[h][:, :], ACT.Copy
                                         ).then_inc(agg_out, 1)
                if known != G - 1:
                    for r in range(R):
                        count_rows(g + 1, C - 1, r)

            passes(group, act)
            for j in range(J):
                post(G - 1, j)

        @block.vector
        def _(dve):
            def low(g, j):
                dve.wait_ge(hi_ready, after(g, J, j + 1))
                nc.vector.tensor_tensor(t_lo[:, j % HL, :], tp[j % TP][:, :], t_hi[:, j % HL, :].bitcast(F32),
                                        ALU.subtract).then_inc(lo_ready, 1)

            def norms(g):
                dve.wait_ge(counted, after(g, R * C, R * C))
                nc.vector.tensor_reduce(sign_row[:, :], sign_sum[:, :, :], AX.X, ALU.add).then_inc(count_step, 1)
                dve.wait_ge(count_step, after(g, COUNT_STEPS, 1))
                nc.vector.tensor_scalar(count[:, :], sign_row[:, :], float(N), 0.5, ALU.add, ALU.mult
                                        ).then_inc(count_step, 1)
                dve.wait_ge(root_ready, g + 1)
                nc.vector.tensor_scalar(norm[:, :], root[:, :], NORM_EPS, None, ALU.max).then_inc(norm_ready, 1)

            def make_inc(g, c, r):
                dve.wait_ge(scaled, after(g, R * C, c * R + r + 1))
                part = inc[:, r, chunk(c)]
                nc.vector.scalar_tensor_tensor(part, part, 0.0, part, ALU.is_gt, ALU.add,
                                               accum_out=degree_part[:, r, c:c + 1]).then_inc(inc_ready, 1)

            def degrees(g):
                dve.wait_ge(inc_ready, after(g, R * C, R * C))
                nc.vector.tensor_reduce(degree[:, :], degree_part[:, :, :], AX.X, ALU.add).then_inc(degree_step, 1)
                dve.wait_ge(degree_step, after(g, 2, 1))
                nc.vector.reciprocal(inv_degree[:, :], degree[:, :]).then_inc(degree_step, 1)

            def merge(st, mean_out, var_out, tmp, step, done, var_done):
                m0, q0, m1, q1 = (st[:, :, n] for n in (1, 2, 4, 5))
                nc.vector.tensor_tensor(tmp[:, 0, :], m0, m1, ALU.add).then_inc(done, 1)
                nc.vector.tensor_tensor(tmp[:, 1, :], m0, m1, ALU.subtract).then_inc(done, 1)
                nc.vector.tensor_tensor(tmp[:, 2, :], q0, q1, ALU.add).then_inc(done, 1)
                step(1)
                nc.vector.tensor_scalar(mean_out[:, :], tmp[:, 0, :], 0.5, None, ALU.mult)
                step(2)
                nc.vector.scalar_tensor_tensor(tmp[:, 1, :], tmp[:, 1, :], 0.25, tmp[:, 1, :], ALU.mult, ALU.mult
                                               ).then_inc(done, 1)
                step(3)
                nc.vector.tensor_scalar(tmp[:, 2, :], tmp[:, 2, :], 1.0 / D, LN_EPS, ALU.mult, ALU.add
                                        ).then_inc(done, 1)
                step(5)
                nc.vector.tensor_tensor(var_out[:, :], tmp[:, 1, :], tmp[:, 2, :], ALU.add).then_inc(var_done, 1)

            def add_aggregate(g, r):
                if r % 2 == 0:
                    dve.wait_ge(agg_back, after(g, 2, r // 2 + 1))
                if r == 0:
                    dve.wait_ge(x_res_landed, after(g, 16, 16))
                    if not (isinstance(g, int) and g == 0):
                        dve.wait_ge(stored, after(g, 32, 0))
                    dve.wait_ge(degree_step, after(g, 2, 2))
                nc.vector.scalar_tensor_tensor(x1[:, r, :], misc[:, (r % 2) * D:(r % 2 + 1) * D],
                                               inv_degree[:, r:r + 1], x_res[:, r, :], ALU.mult, ALU.add
                                               ).then_inc(x1_ready, 1)

            def statistics(g):
                for r in range(R):
                    dve.wait_ge(x1_ready, after(g, R, r + 1))
                    nc.vector.bn_stats(stats[:, r, :], x1[:, r, :]).then_inc(stats_ready, 1)
                dve.wait_ge(stats_ready, after(g, R, R))
                merge(stats, mean, var, parts, lambda n: dve.wait_ge(merge_step, after(g, 5, n)), merge_step, var_ready)

            def normalise(g):
                dve.wait_ge(rstd_ready, g + 1)
                for r in range(R):
                    nc.vector.tensor_scalar(xn2[:, r * D:(r + 1) * D], x1[:, r, :], mean[:, r:r + 1], rstd[:, r:r + 1],
                                            ALU.subtract, ALU.mult).then_inc(xn2_ready, 1)

            def turn_low(g, h):
                dve.wait_ge(x2_hi_ready, after(g, DH, h + 1))
                nc.vector.tensor_tensor(x2_lo[:, h, :], misc[:, :], x2_hi[:, h, :].bitcast(F32), ALU.subtract
                                        ).then_inc(x2_lo_ready, 1)

            wide = lambda a: a[:, :].unsqueeze(2).to_broadcast([P, R, E])

            def gate_exponents(g):
                def step(n):
                    dve.wait_ge(gate_step, after(g, GATE_STEPS, n))

                dve.wait_ge(gate_ready, g + 1)
                nc.vector.tensor_tensor(logits[:, :, :], gate_out[:, :, 0:NE], gate_bias[:, :, :], ALU.add
                                        ).then_inc(gate_step, 1)
                step(1)
                nc.vector.tensor_reduce(top[:, :], logits[:, :, 0:E], AX.X, ALU.max).then_inc(gate_step, 1)
                nc.vector.tensor_scalar(shifted[:, :, E:NE], logits[:, :, E:NE], -1.0, None, ALU.mult
                                        ).then_inc(gate_step, 1)
                step(2)
                nc.vector.tensor_tensor(shifted[:, :, 0:E], logits[:, :, 0:E], wide(top), ALU.subtract
                                        ).then_inc(gate_step, 1)

            def gate_weights(g):
                def step(n):
                    dve.wait_ge(gate_step, after(g, GATE_STEPS, n))

                dve.wait_ge(exp_ready, g + 1)
                nc.vector.tensor_reduce(total[:, :], expd[:, :, 0:E], AX.X, ALU.add).then_inc(gate_step, 1)
                nc.vector.tensor_scalar(thr_den[:, :], expd[:, :, E], 1.0, None, ALU.add).then_inc(gate_step, 1)
                step(5)
                nc.vector.reciprocal(inv_total[:, :], total[:, :]).then_inc(gate_step, 1)
                step(6)
                nc.vector.reciprocal(thr[:, :], thr_den[:, :]).then_inc(gate_step, 1)
                step(7)
                nc.vector.tensor_tensor(adapted[:, :, :], expd[:, :, 0:E], wide(inv_total), ALU.mult
                                        ).then_inc(gate_step, 1)
                step(9)
                nc.vector.scalar_tensor_tensor(adapted[:, :, :], wide(thr), -MAX_THRESHOLD, adapted[:, :, :],
                                               ALU.mult, ALU.add).then_inc(gate_step, 1)
                step(10)
                nc.vector.scalar_tensor_tensor(weight[:, :, :], adapted[:, :, :], 0.0, adapted[:, :, :],
                                               ALU.is_ge, ALU.mult).then_inc(gate_step, 1)
                step(11)
                nc.vector.tensor_reduce(wsum[:, :], weight[:, :, :], AX.X, ALU.add).then_inc(gate_step, 1)
                step(12)
                nc.vector.scalar_tensor_tensor(wsum1[:, :], wsum[:, :], 0.0, wsum[:, :], ALU.is_equal, ALU.add
                                               ).then_inc(gate_step, 1)
                step(13)
                nc.vector.reciprocal(inv_wsum[:, :], wsum1[:, :]).then_inc(gate_step, 1)
                step(14)
                nc.vector.tensor_tensor(weight_n[:, :, :], weight[:, :, :], wide(inv_wsum), ALU.mult
                                        ).then_inc(gate_step, 1)

            def combine(g, r):
                for q in range(ITEMS):
                    dve.wait_ge(experts_ready, after(g, R * ITEMS, r * ITEMS + q + 1))
                    bank = ffn[(r * ITEMS + q) % 2]
                    if q < ITEMS - 1:
                        for n in range(PAIR):
                            e = q * PAIR + n
                            if e > 0:
                                dve.wait_ge(combined, after(g, R * BLOCK_SUMS, r * BLOCK_SUMS + e))
                            nc.vector.scalar_tensor_tensor(x1[:, r, :], bank[:, n * D:(n + 1) * D],
                                                           weight_n[:, r, e:e + 1], x1[:, r, :],
                                                           ALU.mult, ALU.add).then_inc(combined, 1)
                    else:
                        dve.wait_ge(combined, after(g, R * BLOCK_SUMS, r * BLOCK_SUMS + E))
                        nc.vector.tensor_tensor(x1[:, r, :], bank[:, 0:D], x1[:, r, :], ALU.add
                                                ).then_inc(combined, 1)

            def post(g, j):
                for n in range(2):
                    if j == BACK_AT[n] + 1:
                        add_aggregate(g, 2 * n)
                        add_aggregate(g, 2 * n + 1)
                if j == STAT_AT:
                    statistics(g)
                if j == NORMAL_AT:
                    normalise(g)
                for h in range(DH):
                    if j == TURN_AT[h] + 1:
                        turn_low(g, h)
                if j == GATE_AT + 1:
                    gate_exponents(g)
                if j == GATE_AT + 3:
                    gate_weights(g)

            dve.wait_ge(consts_ready, 4)
            for k in range(XC):
                xs = stage[:, k % 2, :].rearrange("p (b d) -> p b d", d=D)
                dve.wait_ge(stage_landed[k % 2], 16 * (k // 2 + 1))
                for b in range(XB):
                    nc.vector.bn_stats(stats0[:, b, :], xs[:, b, :]).then_inc(stats0_ready, 1)
                dve.wait_ge(stats0_ready, (k + 1) * XB)
                merge(stats0, mean0, var0, parts0, lambda n: dve.wait_ge(merge0_step, 5 * k + n), merge0_step,
                      var0_ready)
                dve.wait_ge(rstd0_ready, k + 1)
                for b in range(XB):
                    last = nc.vector.tensor_scalar(xs[:, b, :], xs[:, b, :], mean0[:, b:b + 1], rstd0[:, b:b + 1],
                                                   ALU.subtract, ALU.mult)
                last.then_inc(xn_ready, 1)
                dve.wait_ge(xn_hi_ready, k + 1)
                nc.vector.tensor_tensor(x_part(xn_lo, k), xs, x_part(xn_hi, k).bitcast(F32), ALU.subtract
                                        ).then_inc(xn_lo_ready, 1)

            def group(g, known):
                if has_experts(known):
                    combine(g - 2, 0)
                norms(g)
                for c in range(EARLY):
                    for r in range(R):
                        make_inc(g, c, r)
                    if has_experts(known):
                        combine(g - 2, c + 1)
                for j in range(AHEAD):
                    low(g, j)
                if has_experts(known):
                    combine(g - 2, 3)
                for j in range(J):
                    if j + AHEAD < J:
                        low(g, j + AHEAD)
                    c, r = EARLY + j // R, j % R
                    if c < C:
                        make_inc(g, c, r)
                    if known != 0:
                        post(g - 1, j)
                    if known == 0 and j in WEIGHT_SPLITS:
                        k = WEIGHT_SPLITS.index(j)
                        dve.wait_ge(w_hi_ready, k + 1)
                        nc.vector.tensor_tensor(w_part(w_lo, k), stage[:, k % 2, :], w_part(w_hi, k).bitcast(F32),
                                                ALU.subtract).then_inc(w_lo_ready, 1)
                if known == 0:
                    dve.wait_ge(w_hi_ready, WC + 1)
                    nc.vector.tensor_tensor(gate_lo[:, :, :], gate_raw[:, :, :], gate_hi[:, :, :].bitcast(F32),
                                            ALU.subtract).then_inc(w_lo_ready, 1)
                degrees(g)

            passes(group, dve)
            combine(G - 2, 0)
            for r in range(1, R):
                combine(G - 2, r)
            for j in range(J):
                post(G - 1, j)
            for r in range(R):
                combine(G - 1, r)

        @block.tensor
        def _(pe):
            def turn(g, j):
                if j % CB == 0:
                    pe.wait_ge(inc_ready, after(g, R * C, (j // CB + 1) * R))
                for r in range(R):
                    mm = nc.tensor.transpose(tp[j % TP][:, r * P:(r + 1) * P], inc[:, r, j * P:(j + 1) * P],
                                             ident[:, :])
                mm.then_inc(transposed, 1)

            def multiply(g, known, j):
                pe.wait_ge(lo_ready, after(g, J, j + 1))
                if j == 0 and known != 0:
                    pe.wait_ge(agg_out, after(g - 1, DH, DH))
                for h in range(DH):
                    f = slice(h * P, (h + 1) * P)
                    parts = ((xn_lo, t_hi), (xn_hi, t_lo), (xn_hi, t_hi))
                    for n, (a, b) in enumerate(parts):
                        mm = nc.tensor.matmul(agg[h][:, :], a[:, j, f], b[:, j % HL, :],
                                              start=(j == 0 and n == 0), stop=(j == J - 1 and n == len(parts) - 1))
                mm.then_inc(multiplied, 1)

            def experts(g, r):
                rows = slice(r * P, (r + 1) * P)
                for q in range(ITEMS):
                    n = r * ITEMS + q
                    if n >= 2:
                        rr, qq = divmod(n - 2, ITEMS)
                        pe.wait_ge(combined, after(g, R * BLOCK_SUMS, rr * BLOCK_SUMS + min((qq + 1) * PAIR, E)
                                                   + qq // (ITEMS - 1)))
                    bank = ffn[n % 2]
                    if q < ITEMS - 1:
                        cols = slice(q * PAIR * D, (q + 1) * PAIR * D)
                        parts = [(a, b, h) for h in range(DH)
                                 for a, b in ((x2_lo, w_hi), (x2_hi, w_lo), (x2_hi, w_hi))]
                        for i, (a, b, h) in enumerate(parts):
                            mm = nc.tensor.matmul(bank[:, :], a[:, h, rows], b[:, h, cols],
                                                  start=(i == 0), stop=(i == len(parts) - 1))
                    else:
                        if r == 0:
                            pe.wait_ge(weight_t_ready, g + 1)
                        mm = nc.tensor.matmul(bank[:, 0:D], weight_t[:, rows], bias_sb[:, :], start=True, stop=True)
                    mm.then_inc(experts_ready, 1)

            def post(g, j):
                for n in range(2):
                    if j == BACK_AT[n]:
                        pe.wait_ge(agg_out, after(g, DH, DH))
                        if n == 1:
                            pe.wait_ge(x1_ready, after(g, R, 2))
                        for r in (2 * n, 2 * n + 1):
                            for h in range(DH):
                                col = (r % 2) * D + h * P
                                mm = nc.tensor.transpose(misc[:, col:col + P],
                                                         agg_t[:, h * ROWS + r * P:h * ROWS + (r + 1) * P], ident[:, :])
                        mm.then_inc(agg_back, 1)
                for h in range(DH):
                    if j == TURN_AT[h]:
                        if h == 0:
                            pe.wait_ge(xn2_ready, after(g, R, R))
                        else:
                            pe.wait_ge(x2_lo_ready, after(g, DH, h))
                        for r in range(R):
                            mm = nc.tensor.transpose(misc[:, r * P:(r + 1) * P],
                                                     xn2[:, r * D + h * P:r * D + (h + 1) * P], ident[:, :])
                        mm.then_inc(x2_turned, 1)
                if j == GATE_AT:
                    pe.wait_ge(x2_lo_ready, after(g, DH, DH))
                    parts = [(a, b, h) for h in range(DH)
                             for a, b in ((x2_lo, gate_hi), (x2_hi, gate_lo), (x2_hi, gate_hi))]
                    for r in range(R):
                        for i, (a, b, h) in enumerate(parts):
                            mm = nc.tensor.matmul(gate_out[:, r, :], a[:, h, r * P:(r + 1) * P], b[:, h, :],
                                                  start=(i == 0), stop=(i == len(parts) - 1))
                    mm.then_inc(gate_ready, 1)
                if j == WEIGHT_AT:
                    pe.wait_ge(gate_step, after(g, GATE_STEPS, GATE_STEPS))
                    for r in range(R):
                        mm = nc.tensor.transpose(misc[0:E, r * P:(r + 1) * P], weight_n[:, r, :], ident[:, :])
                    mm.then_inc(weight_turned, 1)

            pe.wait_ge(consts_ready, 4)
            pe.wait_ge(xn_lo_ready, XC)

            def group(g, known):
                if known == 1:
                    pe.wait_ge(w_lo_ready, WC + 1)
                    pe.wait_ge(small_landed, 16 * SMALL_LOADS)
                if has_experts(known):
                    for r in range(R - 1):
                        experts(g - 2, r)
                for j in range(AHEAD):
                    turn(g, j)
                if has_experts(known):
                    experts(g - 2, R - 1)
                for j in range(J):
                    if j + AHEAD < J:
                        turn(g, j + AHEAD)
                    multiply(g, known, j)
                    if known != 0:
                        post(g - 1, j)

            passes(group, pe)
            for r in range(R):
                experts(G - 2, r)
            for j in range(J):
                post(G - 1, j)
            for r in range(R):
                experts(G - 1, r)


_INS = ['x', 'adj', 'L0_ffn_W_gate', 'L0_ffn_b_gate', 'L0_ffn_W_thr', 'L0_ffn_b_thr', 'L0_ffn_W_exp', 'L0_ffn_b_exp']
_OUTS = [((4096, 256), 'float32')]


def kernel(**inputs):
    import numpy as _np
    import concourse.bacc as _bacc
    from concourse import mybir as _mybir
    from concourse.bass_utils import run_bass_kernel_spmd as _run

    nc = _bacc.Bacc("TRN2", target_bir_lowering=False, num_devices=1)
    arrays, args = {}, []
    for name in _INS:
        a = _np.ascontiguousarray(inputs[name])
        arrays[f"in_{name}_dram"] = a
        args.append(nc.dram_tensor(f"in_{name}_dram", a.shape, _mybir.dt.from_np(a.dtype), kind="ExternalInput").ap())
    for i, (shape, dtype) in enumerate(_OUTS):
        dt = _mybir.dt.from_np(_np.dtype(dtype))
        args.append(nc.dram_tensor(f"out_{i}_dram", shape, dt, kind="ExternalOutput").ap())
    program(nc, *args)
    r = _run(nc, [arrays], core_ids=[0])
    return r.results[0]["out_0_dram"]
```

```python
from contextlib import ExitStack

import concourse.bass as bass
from concourse import mybir

F32 = mybir.dt.float32
F32R = mybir.dt.float32r
BF16 = mybir.dt.bfloat16
ALU = mybir.AluOpType
ACT = mybir.ActivationFunctionType
AX = mybir.AxisListType

P = 128
LN_EPS = 1e-5
NORM_EPS = 1e-12
MAX_THRESHOLD = 0.25


def program(nc, x, adj, w_gate, b_gate, w_thr, b_thr, w_exp, b_exp, out):
    N, D = x.shape
    E = w_exp.shape[0]
    DH = D // P
    R = 4
    ROWS = R * P
    G = N // ROWS
    J = N // P
    CB = 4
    C = J // CB
    CW = CB * P
    NE = E + 1
    NEP = E + 2
    XC = 8
    XS = 4
    XB = J // XC
    TP = 2
    WC = 4
    WE = DH * E // WC
    FB = 3
    HL = 4
    AHEAD = 2
    PAIR = 2
    ITEMS = E // PAIR + 1
    BLOCK_SUMS = E + 1
    COUNT_STEPS = 2
    GATE_STEPS = 16
    SMALL_LOADS = 2 * R + 3
    BACK_AT = (9, 12)
    STAT_AT = 14
    NORMAL_AT = 17
    TURN_AT = (20, 23)
    GATE_AT = 25
    WEIGHT_AT = 30
    FIRST_ITEMS = 12
    NORMS_AFTER = 3
    INC_AFTER = (5, 6, 7, 9)
    TURN_AFTER = (8, 10)
    COUNT_AT = 6
    WEIGHT_SPLITS = (8, 9, 22, 24)
    EARLY = 2

    adj_rows = adj.rearrange("(g p r) c -> g p r c", p=P, r=R)
    x_rows = x.rearrange("(g p r) d -> g p r d", p=P, r=R)
    out_rows = out.rearrange("(g p r) d -> g p r d", p=P, r=R)
    x_blocks = x.rearrange("(k b p) d -> k p b d", p=P, b=XB)
    w_rows = w_exp.rearrange("e (h p) f -> h p e f", p=P)

    with ExitStack() as ctx:
        def sb(name, shape, dt=F32):
            return ctx.enter_context(nc.sbuf_tensor(name, shape, dt))

        def ps(name, shape):
            return ctx.enter_context(nc.psum_tensor(name, shape, F32))

        def sem(name):
            return ctx.enter_context(nc.semaphore(name))

        inc = sb("inc", [P, R, N])
        xn_hi = sb("xn_hi", [P, J, D], F32R)
        xn_lo = sb("xn_lo", [P, J, D], F32R)
        w_hi = sb("w_hi", [P, DH, E * D], F32R)
        w_lo = sb("w_lo", [P, DH, E * D], F32R)
        stage = sb("stage", [P, 2, XB * D])
        t_hi = sb("t_hi", [P, HL, ROWS], F32R)
        t_lo = sb("t_lo", [P, HL, ROWS], F32R)
        x_res = sb("x_res", [P, R, D])
        x1 = sb("x1", [P, R, D])
        x2_hi = sb("x2_hi", [P, DH, ROWS], F32R)
        x2_lo = sb("x2_lo", [P, DH, ROWS], F32R)
        signs = sb("signs", [P, 2, CW], BF16)
        ident = sb("ident", [P, P])
        minus_half = sb("minus_half", [P, XB])
        sign_bias = sb("sign_bias", [P, 1])
        half = sb("half", [P, R])
        sign_sum = sb("sign_sum", [P, R, C])
        sign_row = sb("sign_row", [P, R])
        count = sb("count", [P, R])
        root = sb("root", [P, R])
        norm = sb("norm", [P, R])
        degree_part = sb("degree_part", [P, R, C])
        degree = sb("degree", [P, R])
        inv_degree = sb("inv_degree", [P, R])
        stats0 = sb("stats0", [P, XB, 6])
        parts0 = sb("parts0", [P, 3, XB])
        mean0 = sb("mean0", [P, 2, XB])
        var0 = sb("var0", [P, 2, XB])
        rstd0 = sb("rstd0", [P, 2, XB])
        stats = sb("stats", [P, R, 6])
        parts = sb("parts", [P, 3, R])
        mean = sb("mean", [P, R])
        var = sb("var", [P, R])
        rstd = sb("rstd", [P, R])
        gate_raw = sb("gate_raw", [P, DH, NEP])
        gate_w = sb("gate_w", [P, DH, 2 * NEP], F32R)
        gate_bias = sb("gate_bias", [P, R, NE])
        bias_sb = sb("bias_sb", [E, D])
        logits = sb("logits", [P, R, NE])
        top = sb("top", [P, R])
        shifted = sb("shifted", [P, R, NE])
        expd = sb("expd", [P, R, NE])
        total = sb("total", [P, R])
        inv_total = sb("inv_total", [P, R])
        thr_den = sb("thr_den", [P, R])
        thr = sb("thr", [P, R])
        adapted = sb("adapted", [P, R, E])
        weight = sb("weight", [P, R, E])
        wsum = sb("wsum", [P, R])
        wsum1 = sb("wsum1", [P, R])
        inv_wsum = sb("inv_wsum", [P, R])
        weight_n = sb("weight_n", [P, R, E])

        agg_t = stage[:, 0, :]
        xn2 = stage[:, 1, :]
        weight_t = stage[0:E, 1, 0:ROWS]

        x_in = (stage[:, 0, :], stage[:, 1, :], x_res[:, :, :].rearrange("p r d -> p (r d)"),
                x1[:, :, :].rearrange("p r d -> p (r d)"))

        agg = [ps(f"agg{h}", [P, ROWS]) for h in range(DH)]
        tp = [ps(f"tp{k}", [P, ROWS]) for k in range(TP)]
        ffn = [ps(f"ffn{k}", [P, PAIR * D]) for k in range(FB)]
        misc = ps("misc", [P, 512])
        gate_out = misc[:, 0:R * 2 * NEP].rearrange("p (r e) -> p r e", r=R)

        stage_landed = [sem(f"stage_landed{k}") for k in range(XS)]
        adj_landed = [sem(f"adj_landed{c}") for c in range(C)]
        x_res_landed = sem("x_res_landed")
        small_landed = sem("small_landed")
        stored = sem("stored")
        zeroed = sem("zeroed")
        consts_ready = sem("consts_ready")
        var0_ready = sem("var0_ready")
        rstd0_ready = sem("rstd0_ready")
        stats0_ready = sem("stats0_ready")
        merge0_step = sem("merge0_step")
        xn_ready = sem("xn_ready")
        xn_hi_ready = sem("xn_hi_ready")
        xn_lo_ready = sem("xn_lo_ready")
        w_hi_ready = sem("w_hi_ready")
        w_lo_ready = sem("w_lo_ready")
        counted = sem("counted")
        count_step = sem("count_step")
        root_ready = sem("root_ready")
        norm_ready = sem("norm_ready")
        scaled = sem("scaled")
        inc_ready = sem("inc_ready")
        transposed = sem("transposed")
        hi_ready = sem("hi_ready")
        lo_ready = sem("lo_ready")
        multiplied = sem("multiplied")
        degree_step = sem("degree_step")
        agg_out = sem("agg_out")
        agg_back = sem("agg_back")
        x1_ready = sem("x1_ready")
        stats_ready = sem("stats_ready")
        merge_step = sem("merge_step")
        var_ready = sem("var_ready")
        rstd_ready = sem("rstd_ready")
        xn2_ready = sem("xn2_ready")
        x2_turned = sem("x2_turned")
        x2_hi_ready = sem("x2_hi_ready")
        x2_lo_ready = sem("x2_lo_ready")
        gate_ready = sem("gate_ready")
        gate_step = sem("gate_step")
        exp_ready = sem("exp_ready")
        weight_turned = sem("weight_turned")
        weight_t_ready = sem("weight_t_ready")
        experts_ready = sem("experts_ready")
        combined = sem("combined")

        def after(g, per, n):
            return g * per + n

        def x_part(t, k):
            return t[:, k * XB:(k + 1) * XB, :]

        def w_part(t, k):
            h, e = divmod(k * WE, E)
            return t[:, h, e * D:(e + WE) * D]

        def passes(fn, engine):
            for first in range(2):
                fn(first, first)
            with engine.Fori(2, G - 1) as g:
                fn(g, None)
            fn(G - 1, G - 1)

        def has_experts(known):
            return known is None or known >= 2

        def chunk(c):
            return slice(c * CW, (c + 1) * CW)

        def sums(n):
            r, q = divmod(n, ITEMS)
            return r * BLOCK_SUMS + min((q + 1) * PAIR, E) + q // (ITEMS - 1)

        block = ctx.enter_context(nc.Block())

        @block.sync
        def _(sp):
            def load_adj(g, c):
                sp.dma_start(inc[:, :, chunk(c)], adj_rows[g, :, :, chunk(c)]).then_inc(adj_landed[c], 16)

            def load_x_res(g):
                sp.dma_start(x_res[:, :, :], x_rows[g]).then_inc(x_res_landed, 16)

            def store(g, half):
                sp.wait_ge(combined, after(g, R * BLOCK_SUMS, (2 * half + 2) * BLOCK_SUMS))
                sp.dma_start(out_rows[g, :, 2 * half:2 * half + 2, :],
                             x1[:, 2 * half:2 * half + 2, :]).then_inc(stored, 16)

            for k in range(XC):
                if k >= XS:
                    sp.wait_ge(xn_hi_ready, k - XS + 1)
                    sp.wait_ge(xn_lo_ready, k - XS + 1)
                sp.dma_start(x_in[k % XS].rearrange("p (b d) -> p b d", d=D), x_blocks[k]
                             ).then_inc(stage_landed[k % XS], 16)
                if k >= XS - 1:
                    load_adj(0, k - XS + 1)
            for c in range(XC - XS + 1, C):
                load_adj(0, c)
            sp.wait_ge(xn_hi_ready, XC)
            sp.wait_ge(xn_lo_ready, XC)
            load_x_res(0)
            for e in range(R):
                sp.dma_start(gate_bias[:, e, 0:E], b_gate.rearrange("(a e) -> a e", a=1).to_broadcast([P, E])
                             ).then_inc(small_landed, 16)
                sp.dma_start(gate_bias[:, e, E:NE], b_thr.rearrange("(a e) -> a e", a=1).to_broadcast([P, 1])
                             ).then_inc(small_landed, 16)
            sp.dma_start(bias_sb[:, :], b_exp).then_inc(small_landed, 16)
            sp.wait_ge(zeroed, 1)
            with nc.allow_non_contiguous_dma(reason="gate weights of a few bytes a row"):
                sp.dma_start(gate_raw[:, :, 0:E], w_gate.rearrange("(h p) e -> p h e", p=P)
                             ).then_inc(small_landed, 16)
                sp.dma_start(gate_raw[:, :, E:NE], w_thr.rearrange("(h p) e -> p h e", p=P)
                             ).then_inc(small_landed, 16)

            def load_weights(k):
                if k >= 2:
                    sp.wait_ge(w_hi_ready, k - 1)
                    sp.wait_ge(w_lo_ready, k - 1)
                h, e = divmod(k * WE, E)
                sp.dma_start(stage[:, k % 2, :].rearrange("p (e f) -> p e f", e=WE),
                             w_rows[h, :, e:e + WE, :]).then_inc(stage_landed[k % 2], 16)

            for k in range(2):
                load_weights(k)

            def group(g, known):
                if has_experts(known):
                    store(g - 2, 0)
                for c in range(C):
                    if known != G - 1:
                        sp.wait_ge(transposed, after(g, J, (c + 1) * CB))
                        load_adj(g + 1, c)
                    if c == 1 and has_experts(known):
                        store(g - 2, 1)
                    if c == C // 2 and known == 0:
                        for k in range(2, WC):
                            load_weights(k)
                    if c == C // 2 and known != 0:
                        sp.wait_ge(x1_ready, after(g - 1, R, R))
                        load_x_res(g)

            passes(group, sp)
            for g in (G - 2, G - 1):
                for half in range(2):
                    store(g, half)
            sp.wait_ge(stored, 16 * 2 * G)

        @block.gpsimd
        def _(pool):
            nc.gpsimd.memset(gate_raw[:, :, :], 0.0).then_inc(zeroed, 1)
            nc.gpsimd.memset(ident[:, :], 0.0).then_inc(zeroed, 1)
            nc.gpsimd.memset(minus_half[:, :], -0.5).then_inc(consts_ready, 1)
            nc.gpsimd.memset(half[:, :], 0.5).then_inc(consts_ready, 1)
            nc.gpsimd.memset(sign_bias[:, :], -2.0 ** -120).then_inc(consts_ready, 1)
            pool.wait_ge(zeroed, 2)
            nc.gpsimd.affine_select(out=ident[:, :], in_=ident[:, :], compare_op=ALU.not_equal, fill=1.0,
                                    base=0, pattern=[[-1, P]], channel_multiplier=1).then_inc(consts_ready, 1)
            pool.wait_ge(consts_ready, 4)
            def first_low(k):
                pool.wait_ge(xn_hi_ready, k + 1)
                nc.gpsimd.tensor_tensor(x_part(xn_lo, k), x_in[k % XS].rearrange("p (b d) -> p b d", d=D),
                                        x_part(xn_hi, k).bitcast(F32), ALU.subtract).then_inc(xn_lo_ready, 1)

            for k in range(XC):
                pool.wait_ge(var0_ready, k + 1)
                nc.gpsimd.tensor_tensor(rstd0[:, k % 2, :], var0[:, k % 2, :], minus_half[:, 0:XB], ALU.pow
                                        ).then_inc(rstd0_ready, 1)
                if k >= 1:
                    first_low(k - 1)
            first_low(XC - 1)

            def scale_rows(g, c, r):
                if c == 0 and r == 0:
                    pool.wait_ge(norm_ready, g + 1)
                    nc.gpsimd.tensor_tensor(inc[:, r, chunk(c)], inc[:, r, chunk(c)],
                                            norm[:, r:r + 1].to_broadcast([P, CW]), ALU.mult).then_inc(scaled, 1)
                else:
                    nc.gpsimd.tensor_scalar(inc[:, r, chunk(c)], inc[:, r, chunk(c)], norm[:, r:r + 1], 1.0,
                                            ALU.mult, ALU.mult).then_inc(scaled, 1)

            def group(g, known):
                pool.wait_ge(count_step, after(g, COUNT_STEPS, 2))
                nc.gpsimd.tensor_tensor(root[:, :], count[:, :], half[:, :], ALU.pow).then_inc(root_ready, 1)
                for c in range(C):
                    for r in range(R):
                        scale_rows(g, c, r)
                if known != 0:
                    inverse_deviation(g - 1)

            def inverse_deviation(g):
                pool.wait_ge(var_ready, g + 1)
                nc.gpsimd.tensor_tensor(rstd[:, :], var[:, :], minus_half[:, 0:R], ALU.pow
                                        ).then_inc(rstd_ready, 1)

            passes(group, pool)
            inverse_deviation(G - 1)

        @block.scalar
        def _(act):
            def count_rows(g, c, r):
                if r == 0:
                    act.wait_ge(adj_landed[c], after(g, 16, 16))
                if r % 2 == 0 and not (isinstance(g, int) and g * C + c + r == 0):
                    act.wait_ge(counted, after(g, R * C, c * R + r))
                nc.scalar.activation(signs[:, r % 2, :], inc[:, r, chunk(c)], ACT.Sign,
                                     bias=sign_bias[:, 0:1], scale=2.0 ** 100,
                                     accum_out=sign_sum[:, r, c:c + 1]).then_inc(counted, 1)

            def high(g, known, j):
                act.wait_ge(transposed, after(g, J, j + 1))
                if j >= HL:
                    act.wait_ge(multiplied, after(g, J, j - HL + 1))
                elif known != 0:
                    act.wait_ge(multiplied, after(g, J, j - HL + 1))
                nc.scalar.activation(t_hi[:, j % HL, :], tp[j % TP][:, :], ACT.Copy).then_inc(hi_ready, 1)

            def split_weights(k):
                act.wait_ge(stage_landed[k % 2], 16 * (XC // XS + k // 2 + 1))
                nc.scalar.activation(w_part(w_hi, k), stage[:, k % 2, :], ACT.Copy).then_inc(w_hi_ready, 1)

            def post(g, j):
                for h in range(DH):
                    if j == TURN_AT[h] + 1:
                        act.wait_ge(x2_turned, after(g, DH, h + 1))
                        nc.scalar.activation(x2_hi[:, h, :], misc[:, :], ACT.Copy).then_inc(x2_hi_ready, 1)
                if j == GATE_AT + 2:
                    act.wait_ge(gate_step, after(g, GATE_STEPS, 5))
                    nc.scalar.activation(expd[:, :, :], shifted[:, :, :], ACT.Exp).then_inc(exp_ready, 1)
                if j == WEIGHT_AT + 1:
                    act.wait_ge(weight_turned, g + 1)
                    nc.scalar.activation(weight_t, misc[0:E, :], ACT.Copy).then_inc(weight_t_ready, 1)

            act.wait_ge(consts_ready, 4)
            for k in range(XC):
                act.wait_ge(xn_ready, k + 1)
                nc.scalar.activation(x_part(xn_hi, k), x_in[k % XS].rearrange("p (b d) -> p b d", d=D),
                                     ACT.Copy).then_inc(xn_hi_ready, 1)
                if k >= 2:
                    for r in range(R):
                        count_rows(0, k - 2, r)
            for c in range(XC - 2, C):
                for r in range(R):
                    count_rows(0, c, r)

            def group(g, known):
                for j in range(AHEAD):
                    high(g, known, j)
                for j in range(J):
                    if j + AHEAD < J:
                        high(g, known, j + AHEAD)
                    n = j - COUNT_AT
                    if 0 <= n < (C - 2) * R and known != G - 1:
                        if n == 0:
                            act.wait_ge(count_step, after(g, COUNT_STEPS, 1))
                        count_rows(g + 1, n // R, n % R)
                    if known != 0:
                        post(g - 1, j)
                    if known == 0 and j in WEIGHT_SPLITS:
                        split_weights(WEIGHT_SPLITS.index(j))
                if known == 0:
                    act.wait_ge(small_landed, 16 * SMALL_LOADS)
                    nc.scalar.activation(gate_w[:, :, 0:NEP], gate_raw[:, :, :], ACT.Copy).then_inc(w_hi_ready, 1)
                if known != G - 1:
                    for r in range(R):
                        count_rows(g + 1, C - 2, r)
                act.wait_ge(multiplied, after(g, J, J))
                for h in range(DH):
                    if known != 0 and h == 0:
                        act.wait_ge(agg_back, after(g - 1, 2, 2))
                    nc.scalar.activation(agg_t[:, h * ROWS:(h + 1) * ROWS], agg[h][:, :], ACT.Copy
                                         ).then_inc(agg_out, 1)
                if known != G - 1:
                    for r in range(R):
                        count_rows(g + 1, C - 1, r)

            passes(group, act)
            for j in range(J):
                post(G - 1, j)

        @block.vector
        def _(dve):
            def low(g, j):
                dve.wait_ge(hi_ready, after(g, J, j + 1))
                nc.vector.tensor_tensor(t_lo[:, j % HL, :], tp[j % TP][:, :], t_hi[:, j % HL, :].bitcast(F32),
                                        ALU.subtract).then_inc(lo_ready, 1)

            def norms(g):
                dve.wait_ge(counted, after(g, R * C, R * C))
                nc.vector.tensor_reduce(sign_row[:, :], sign_sum[:, :, :], AX.X, ALU.add).then_inc(count_step, 1)
                dve.wait_ge(count_step, after(g, COUNT_STEPS, 1))
                nc.vector.tensor_scalar(count[:, :], sign_row[:, :], float(N), 0.5, ALU.add, ALU.mult
                                        ).then_inc(count_step, 1)
                dve.wait_ge(root_ready, g + 1)
                nc.vector.tensor_scalar(norm[:, :], root[:, :], NORM_EPS, None, ALU.max).then_inc(norm_ready, 1)

            def make_inc(g, c, r):
                dve.wait_ge(scaled, after(g, R * C, c * R + r + 1))
                part = inc[:, r, chunk(c)]
                nc.vector.scalar_tensor_tensor(part, part, 0.0, part, ALU.is_gt, ALU.add,
                                               accum_out=degree_part[:, r, c:c + 1]).then_inc(inc_ready, 1)

            def degrees(g):
                dve.wait_ge(inc_ready, after(g, R * C, R * C))
                nc.vector.tensor_reduce(degree[:, :], degree_part[:, :, :], AX.X, ALU.add).then_inc(degree_step, 1)
                dve.wait_ge(degree_step, after(g, 2, 1))
                nc.vector.reciprocal(inv_degree[:, :], degree[:, :]).then_inc(degree_step, 1)

            def merge(st, mean_out, var_out, tmp, step, done, var_done):
                m0, q0, m1, q1 = (st[:, :, n] for n in (1, 2, 4, 5))
                nc.vector.tensor_tensor(tmp[:, 0, :], m0, m1, ALU.add).then_inc(done, 1)
                nc.vector.tensor_tensor(tmp[:, 1, :], m0, m1, ALU.subtract).then_inc(done, 1)
                nc.vector.tensor_tensor(tmp[:, 2, :], q0, q1, ALU.add).then_inc(done, 1)
                step(1)
                nc.vector.tensor_scalar(mean_out, tmp[:, 0, :], 0.5, None, ALU.mult)
                step(2)
                nc.vector.scalar_tensor_tensor(tmp[:, 1, :], tmp[:, 1, :], 0.25, tmp[:, 1, :], ALU.mult, ALU.mult
                                               ).then_inc(done, 1)
                step(3)
                nc.vector.tensor_scalar(tmp[:, 2, :], tmp[:, 2, :], 1.0 / D, LN_EPS, ALU.mult, ALU.add
                                        ).then_inc(done, 1)
                step(5)
                nc.vector.tensor_tensor(var_out, tmp[:, 1, :], tmp[:, 2, :], ALU.add).then_inc(var_done, 1)

            def add_aggregate(g, r):
                if r % 2 == 0:
                    dve.wait_ge(agg_back, after(g, 2, r // 2 + 1))
                if r == 0:
                    dve.wait_ge(x_res_landed, after(g, 16, 16))
                    if not (isinstance(g, int) and g == 0):
                        dve.wait_ge(stored, after(g, 32, 0))
                    dve.wait_ge(degree_step, after(g, 2, 2))
                nc.vector.scalar_tensor_tensor(x1[:, r, :], misc[:, (r % 2) * D:(r % 2 + 1) * D],
                                               inv_degree[:, r:r + 1], x_res[:, r, :], ALU.mult, ALU.add
                                               ).then_inc(x1_ready, 1)

            def statistics(g):
                for r in range(R):
                    dve.wait_ge(x1_ready, after(g, R, r + 1))
                    nc.vector.bn_stats(stats[:, r, :], x1[:, r, :]).then_inc(stats_ready, 1)
                dve.wait_ge(stats_ready, after(g, R, R))
                merge(stats, mean[:, :], var[:, :], parts, lambda n: dve.wait_ge(merge_step, after(g, 5, n)), merge_step, var_ready)

            def normalise(g):
                dve.wait_ge(rstd_ready, g + 1)
                for r in range(R):
                    nc.vector.tensor_scalar(xn2[:, r * D:(r + 1) * D], x1[:, r, :], mean[:, r:r + 1], rstd[:, r:r + 1],
                                            ALU.subtract, ALU.mult).then_inc(xn2_ready, 1)

            def turn_low(g, h):
                dve.wait_ge(x2_hi_ready, after(g, DH, h + 1))
                nc.vector.tensor_tensor(x2_lo[:, h, :], misc[:, :], x2_hi[:, h, :].bitcast(F32), ALU.subtract
                                        ).then_inc(x2_lo_ready, 1)

            wide = lambda a: a[:, :].unsqueeze(2).to_broadcast([P, R, E])

            def gate_exponents(g):
                def step(n):
                    dve.wait_ge(gate_step, after(g, GATE_STEPS, n))

                dve.wait_ge(gate_ready, g + 1)
                nc.vector.tensor_tensor(logits[:, :, :], gate_out[:, :, 0:NE], gate_bias[:, :, :], ALU.add
                                        ).then_inc(gate_step, 1)
                step(1)
                nc.vector.tensor_tensor(logits[:, :, :], gate_out[:, :, NEP:NEP + NE], logits[:, :, :], ALU.add
                                        ).then_inc(gate_step, 1)
                step(2)
                nc.vector.tensor_reduce(top[:, :], logits[:, :, 0:E], AX.X, ALU.max).then_inc(gate_step, 1)
                nc.vector.tensor_scalar(shifted[:, :, E:NE], logits[:, :, E:NE], -1.0, None, ALU.mult
                                        ).then_inc(gate_step, 1)
                step(3)
                nc.vector.tensor_tensor(shifted[:, :, 0:E], logits[:, :, 0:E], wide(top), ALU.subtract
                                        ).then_inc(gate_step, 1)

            def gate_weights(g):
                def step(n):
                    dve.wait_ge(gate_step, after(g, GATE_STEPS, n))

                dve.wait_ge(exp_ready, g + 1)
                nc.vector.tensor_reduce(total[:, :], expd[:, :, 0:E], AX.X, ALU.add).then_inc(gate_step, 1)
                nc.vector.tensor_scalar(thr_den[:, :], expd[:, :, E], 1.0, None, ALU.add).then_inc(gate_step, 1)
                step(6)
                nc.vector.reciprocal(inv_total[:, :], total[:, :]).then_inc(gate_step, 1)
                step(7)
                nc.vector.reciprocal(thr[:, :], thr_den[:, :]).then_inc(gate_step, 1)
                step(8)
                nc.vector.tensor_tensor(adapted[:, :, :], expd[:, :, 0:E], wide(inv_total), ALU.mult
                                        ).then_inc(gate_step, 1)
                step(10)
                nc.vector.scalar_tensor_tensor(adapted[:, :, :], wide(thr), -MAX_THRESHOLD, adapted[:, :, :],
                                               ALU.mult, ALU.add).then_inc(gate_step, 1)
                step(11)
                nc.vector.scalar_tensor_tensor(weight[:, :, :], adapted[:, :, :], 0.0, adapted[:, :, :],
                                               ALU.is_ge, ALU.mult).then_inc(gate_step, 1)
                step(12)
                nc.vector.tensor_reduce(wsum[:, :], weight[:, :, :], AX.X, ALU.add).then_inc(gate_step, 1)
                step(13)
                nc.vector.scalar_tensor_tensor(wsum1[:, :], wsum[:, :], 0.0, wsum[:, :], ALU.is_equal, ALU.add
                                               ).then_inc(gate_step, 1)
                step(14)
                nc.vector.reciprocal(inv_wsum[:, :], wsum1[:, :]).then_inc(gate_step, 1)
                step(15)
                nc.vector.tensor_tensor(weight_n[:, :, :], weight[:, :, :], wide(inv_wsum), ALU.mult
                                        ).then_inc(gate_step, 1)

            def combine(g, n, acc):
                r, q = divmod(n, ITEMS)
                dve.wait_ge(experts_ready, after(g, R * ITEMS, n + 1))
                bank = ffn[n % FB]
                if q < ITEMS - 1:
                    for i in range(PAIR):
                        e = q * PAIR + i
                        if e > 0:
                            dve.wait_ge(combined, after(g, R * BLOCK_SUMS, r * BLOCK_SUMS + e))
                        nc.vector.scalar_tensor_tensor(acc[:, r, :], bank[:, i * D:(i + 1) * D],
                                                       weight_n[:, r, e:e + 1], acc[:, r, :],
                                                       ALU.mult, ALU.add).then_inc(combined, 1)
                else:
                    dve.wait_ge(combined, after(g, R * BLOCK_SUMS, r * BLOCK_SUMS + E))
                    nc.vector.tensor_tensor(acc[:, r, :], bank[:, 0:D], acc[:, r, :], ALU.add
                                            ).then_inc(combined, 1)

            def post(g, j):
                for n in range(2):
                    if j == BACK_AT[n] + 1:
                        add_aggregate(g, 2 * n)
                        add_aggregate(g, 2 * n + 1)
                if j == STAT_AT:
                    statistics(g)
                if j == NORMAL_AT:
                    normalise(g)
                for h in range(DH):
                    if j == TURN_AT[h] + 1:
                        turn_low(g, h)
                if j == GATE_AT + 1:
                    gate_exponents(g)
                if j == GATE_AT + 3:
                    gate_weights(g)

            dve.wait_ge(consts_ready, 4)
            def first_statistics(k):
                xs = x_in[k % XS].rearrange("p (b d) -> p b d", d=D)
                dve.wait_ge(stage_landed[k % XS], 16 * (k // XS + 1))
                for b in range(XB):
                    nc.vector.bn_stats(stats0[:, b, :], xs[:, b, :]).then_inc(stats0_ready, 1)
                dve.wait_ge(stats0_ready, (k + 1) * XB)
                merge(stats0, mean0[:, k % 2, :], var0[:, k % 2, :], parts0,
                      lambda n: dve.wait_ge(merge0_step, 5 * k + n), merge0_step, var0_ready)

            def first_normalise(k):
                xs = x_in[k % XS].rearrange("p (b d) -> p b d", d=D)
                dve.wait_ge(rstd0_ready, k + 1)
                for b in range(XB):
                    last = nc.vector.tensor_scalar(xs[:, b, :], xs[:, b, :], mean0[:, k % 2, b:b + 1],
                                                   rstd0[:, k % 2, b:b + 1], ALU.subtract, ALU.mult)
                last.then_inc(xn_ready, 1)

            first_statistics(0)
            for k in range(1, XC):
                first_statistics(k)
                first_normalise(k - 1)
            first_normalise(XC - 1)

            def group(g, known):
                for n in range(FIRST_ITEMS):
                    if has_experts(known):
                        combine(g - 2, n, x1)
                    if n == NORMS_AFTER:
                        norms(g)
                    if n in INC_AFTER:
                        part = INC_AFTER.index(n)
                        for r in range(R // 2):
                            make_inc(g, part // 2, part % 2 * R // 2 + r)
                    if n in TURN_AFTER:
                        low(g, TURN_AFTER.index(n))
                for j in range(J):
                    if j + AHEAD < J:
                        low(g, j + AHEAD)
                    c, r = EARLY + j // R, j % R
                    if c < C:
                        make_inc(g, c, r)
                    if has_experts(known) and FIRST_ITEMS + j < R * ITEMS:
                        combine(g - 2, FIRST_ITEMS + j, x1)
                    if known != 0:
                        post(g - 1, j)
                    if known == 0 and j in WEIGHT_SPLITS:
                        k = WEIGHT_SPLITS.index(j)
                        dve.wait_ge(w_hi_ready, k + 1)
                        nc.vector.tensor_tensor(w_part(w_lo, k), stage[:, k % 2, :], w_part(w_hi, k).bitcast(F32),
                                                ALU.subtract).then_inc(w_lo_ready, 1)
                if known == 0:
                    dve.wait_ge(w_hi_ready, WC + 1)
                    nc.vector.tensor_tensor(gate_w[:, :, NEP:2 * NEP], gate_raw[:, :, :],
                                            gate_w[:, :, 0:NEP].bitcast(F32), ALU.subtract).then_inc(w_lo_ready, 1)
                degrees(g)

            passes(group, dve)
            for n in range(R * ITEMS):
                combine(G - 2, n, x1)
            for j in range(J):
                post(G - 1, j)
            for n in range(R * ITEMS):
                combine(G - 1, n, x1)

        @block.tensor
        def _(pe):
            def turn(g, j):
                if j % CB == 0:
                    pe.wait_ge(inc_ready, after(g, R * C, (j // CB + 1) * R))
                if j >= TP:
                    pe.wait_ge(lo_ready, after(g, J, j - TP + 1))
                for r in range(R):
                    mm = nc.tensor.transpose(tp[j % TP][:, r * P:(r + 1) * P], inc[:, r, j * P:(j + 1) * P],
                                             ident[:, :])
                mm.then_inc(transposed, 1)

            def multiply(g, known, j):
                pe.wait_ge(lo_ready, after(g, J, j + 1))
                if j == 0 and known != 0:
                    pe.wait_ge(agg_out, after(g - 1, DH, DH))
                for h in range(DH):
                    f = slice(h * P, (h + 1) * P)
                    parts = ((xn_lo, t_hi), (xn_hi, t_lo), (xn_hi, t_hi))
                    for n, (a, b) in enumerate(parts):
                        mm = nc.tensor.matmul(agg[h][:, :], a[:, j, f], b[:, j % HL, :],
                                              start=(j == 0 and n == 0), stop=(j == J - 1 and n == len(parts) - 1))
                mm.then_inc(multiplied, 1)

            def experts(g, n):
                r, q = divmod(n, ITEMS)
                rows = slice(r * P, (r + 1) * P)
                if n >= FB:
                    pe.wait_ge(combined, after(g, R * BLOCK_SUMS, sums(n - FB)))
                bank = ffn[n % FB]
                if q < ITEMS - 1:
                    cols = slice(q * PAIR * D, (q + 1) * PAIR * D)
                    parts = [(a, b, h) for h in range(DH)
                             for a, b in ((x2_lo, w_hi), (x2_hi, w_lo), (x2_hi, w_hi))]
                    for i, (a, b, h) in enumerate(parts):
                        mm = nc.tensor.matmul(bank[:, :], a[:, h, rows], b[:, h, cols],
                                              start=(i == 0), stop=(i == len(parts) - 1))
                else:
                    if r == 0:
                        pe.wait_ge(weight_t_ready, g + 1)
                    mm = nc.tensor.matmul(bank[:, 0:D], weight_t[:, rows], bias_sb[:, :], start=True, stop=True)
                mm.then_inc(experts_ready, 1)

            def post(g, j):
                for n in range(2):
                    if j == BACK_AT[n]:
                        pe.wait_ge(agg_out, after(g, DH, DH))
                        if n == 1:
                            pe.wait_ge(x1_ready, after(g, R, 2))
                        for r in (2 * n, 2 * n + 1):
                            for h in range(DH):
                                col = (r % 2) * D + h * P
                                mm = nc.tensor.transpose(misc[:, col:col + P],
                                                         agg_t[:, h * ROWS + r * P:h * ROWS + (r + 1) * P], ident[:, :])
                        mm.then_inc(agg_back, 1)
                for h in range(DH):
                    if j == TURN_AT[h]:
                        if h == 0:
                            pe.wait_ge(xn2_ready, after(g, R, R))
                        else:
                            pe.wait_ge(x2_lo_ready, after(g, DH, h))
                        for r in range(R):
                            mm = nc.tensor.transpose(misc[:, r * P:(r + 1) * P],
                                                     xn2[:, r * D + h * P:r * D + (h + 1) * P], ident[:, :])
                        mm.then_inc(x2_turned, 1)
                if j == GATE_AT:
                    pe.wait_ge(x2_lo_ready, after(g, DH, DH))
                    parts = [(a, gate_w, h) for h in range(DH) for a in (x2_lo, x2_hi)]
                    for r in range(R):
                        for i, (a, b, h) in enumerate(parts):
                            mm = nc.tensor.matmul(gate_out[:, r, :], a[:, h, r * P:(r + 1) * P], b[:, h, :],
                                                  start=(i == 0), stop=(i == len(parts) - 1))
                    mm.then_inc(gate_ready, 1)
                if j == WEIGHT_AT:
                    pe.wait_ge(gate_step, after(g, GATE_STEPS, GATE_STEPS))
                    for r in range(R):
                        mm = nc.tensor.transpose(misc[0:E, r * P:(r + 1) * P], weight_n[:, r, :], ident[:, :])
                    mm.then_inc(weight_turned, 1)

            pe.wait_ge(consts_ready, 4)
            pe.wait_ge(xn_lo_ready, XC)

            def group(g, known):
                if known == 1:
                    pe.wait_ge(w_lo_ready, WC + 1)
                    pe.wait_ge(small_landed, 16 * SMALL_LOADS)
                for n in range(FIRST_ITEMS):
                    if has_experts(known):
                        experts(g - 2, n)
                    if n in TURN_AFTER:
                        turn(g, TURN_AFTER.index(n))
                for j in range(J):
                    if j + AHEAD < J:
                        turn(g, j + AHEAD)
                    multiply(g, known, j)
                    if has_experts(known) and FIRST_ITEMS + j < R * ITEMS:
                        experts(g - 2, FIRST_ITEMS + j)
                    if known != 0:
                        post(g - 1, j)

            passes(group, pe)
            for n in range(R * ITEMS):
                experts(G - 2, n)
            for j in range(J):
                post(G - 1, j)
            for n in range(R * ITEMS):
                experts(G - 1, n)


_INS = ['x', 'adj', 'L0_ffn_W_gate', 'L0_ffn_b_gate', 'L0_ffn_W_thr', 'L0_ffn_b_thr', 'L0_ffn_W_exp', 'L0_ffn_b_exp']
_OUTS = [((4096, 256), 'float32')]


def kernel(**inputs):
    import numpy as _np
    import concourse.bacc as _bacc
    from concourse import mybir as _mybir
    from concourse.bass_utils import run_bass_kernel_spmd as _run

    nc = _bacc.Bacc("TRN2", target_bir_lowering=False, num_devices=1)
    arrays, args = {}, []
    for name in _INS:
        a = _np.ascontiguousarray(inputs[name])
        arrays[f"in_{name}_dram"] = a
        args.append(nc.dram_tensor(f"in_{name}_dram", a.shape, _mybir.dt.from_np(a.dtype), kind="ExternalInput").ap())
    for i, (shape, dtype) in enumerate(_OUTS):
        dt = _mybir.dt.from_np(_np.dtype(dtype))
        args.append(nc.dram_tensor(f"out_{i}_dram", shape, dt, kind="ExternalOutput").ap())
    program(nc, *args)
    r = _run(nc, [arrays], core_ids=[0])
    return r.results[0]["out_0_dram"]
```

```python
from contextlib import ExitStack

from concourse import mybir

F32 = mybir.dt.float32
F32R = mybir.dt.float32r
BF16 = mybir.dt.bfloat16
ALU = mybir.AluOpType
ACT = mybir.ActivationFunctionType
AX = mybir.AxisListType

P = 128
LN_EPS = 1e-5
NORM_EPS = 1e-12
MAX_THRESHOLD = 0.25


def program(nc, x, adj, w_gate, b_gate, w_thr, b_thr, w_exp, b_exp, out):
    N, D = x.shape
    E = w_exp.shape[0]
    DH = D // P
    R = 4
    ROWS = R * P
    G = N // ROWS
    J = N // P
    CB = 4
    C = J // CB
    CW = CB * P
    NE = E + 1
    NEP = E + 2
    XC = 8
    XS = 4
    XB = J // XC
    TP = 2
    WC = 4
    WE = DH * E // WC
    FB = 3
    HL = 4
    AHEAD = 2
    PAIR = 2
    ITEMS = E // PAIR + 1
    BLOCK_SUMS = E + 1
    WEIGHT_LOADED = 3
    COUNT_STEPS = 2
    GATE_STEPS = 19
    SMALL_LOADS = 2 * R + 2
    BIAS_PARTS = 3
    PART = 32
    STACK = (BIAS_PARTS - 1) * PART + E

    FIRST_ITEMS = 12
    COUNT_AFTER = 0
    NORMS_AFTER = 2
    INC_AFTER = (5, 5, 6, 6, 9, 10)
    TURN_AFTER = (8, 9)
    EARLY = 2
    ACT_ROWS = R // 2
    COUNT_AT = 6
    DVE_ROWS = R // 2

    BACK_AT = (9, 11)
    STAT_AT = (11, 13)
    MERGE_AT = 14
    NORMAL_AT = (15, 16)
    TURN_AT = (18, 20)
    GATE_AT = 22
    WEIGHT_AT = 29
    LAST_FROM = 9

    LATE_X = 4
    LATE_AT = (0, 6, 12, 18)
    MERGE_STEP = 2
    NORMAL_STEPS = (4, 5)
    SPLIT_STEP = 6
    LATE_CHUNK = 2
    WEIGHT_LOADS = (3, 6)
    WEIGHT_SPLITS = (24, 26, 28, 30)
    SMALL_SPLIT_AT = 5

    adj_rows = adj.rearrange("(g p r) c -> g p r c", p=P, r=R)
    x_rows = x.rearrange("(g p r) d -> g p r d", p=P, r=R)
    out_rows = out.rearrange("(g p r) d -> g p r d", p=P, r=R)
    x_blocks = x.rearrange("(k b p) d -> k p b d", p=P, b=XB)
    w_rows = w_exp.rearrange("e (h p) f -> h p e f", p=P)

    with ExitStack() as ctx:
        def sb(name, shape, dt=F32):
            return ctx.enter_context(nc.sbuf_tensor(name, shape, dt))

        def ps(name, shape):
            return ctx.enter_context(nc.psum_tensor(name, shape, F32))

        def sem(name):
            return ctx.enter_context(nc.semaphore(name))

        inc = sb("inc", [P, R, N])
        xn_hi = sb("xn_hi", [P, J, D], F32R)
        xn_lo = sb("xn_lo", [P, J, D], F32R)
        w_hi = sb("w_hi", [P, DH, E * D], F32R)
        w_lo = sb("w_lo", [P, DH, E * D], F32R)
        stage = sb("stage", [P, 2, XB * D])
        t_hi = sb("t_hi", [P, HL, ROWS], F32R)
        t_lo = sb("t_lo", [P, HL, ROWS], F32R)
        x_res = sb("x_res", [P, R, D])
        x1 = sb("x1", [P, R, D])
        x2_hi = sb("x2_hi", [P, DH, ROWS], F32R)
        x2_lo = sb("x2_lo", [P, DH, ROWS], F32R)
        signs = sb("signs", [P, CW], BF16)
        ident = sb("ident", [P, P])
        minus_half = sb("minus_half", [P, XB])
        sign_bias = sb("sign_bias", [P, 1])
        half = sb("half", [P, R])
        sign_sum = sb("sign_sum", [P, R, C])
        sign_row = sb("sign_row", [P, R])
        count = sb("count", [P, R])
        root = sb("root", [P, R])
        norm = sb("norm", [P, R])
        degree_part = sb("degree_part", [P, R, C])
        degree = sb("degree", [P, R])
        inv_degree = sb("inv_degree", [P, R])
        stats0 = sb("stats0", [P, XB, 6])
        parts0 = sb("parts0", [P, 3, XB])
        mean0 = sb("mean0", [P, 2, XB])
        var0 = sb("var0", [P, 2, XB])
        rstd0 = sb("rstd0", [P, 2, XB])
        stats = sb("stats", [P, R, 6])
        parts = sb("parts", [P, 3, R])
        mean = sb("mean", [P, R])
        var = sb("var", [P, R])
        rstd = sb("rstd", [P, R])
        gate_raw = sb("gate_raw", [P, DH, NEP])
        gate_w = sb("gate_w", [P, DH, 2 * NEP], F32R)
        gate_bias = sb("gate_bias", [P, R, NE])
        bias_parts = sb("bias_parts", [STACK, D], F32R)
        weight_parts = sb("weight_parts", [P, R, STACK], F32R)
        weight_t = sb("weight_t", [STACK, ROWS], F32R)[:, :]
        logits = sb("logits", [P, R, NE])
        top = sb("top", [P, R])
        expd = sb("expd", [P, R, NE])
        total = sb("total", [P, R])
        inv_total = sb("inv_total", [P, R])
        thr = sb("thr", [P, R])
        weight = sb("weight", [P, R, E])
        wsum = sb("wsum", [P, R])
        inv_wsum = sb("inv_wsum", [P, R])
        weight_n = sb("weight_n", [P, R, E])[:, :, :]

        agg_t = stage[:, 0, :]
        xn2 = stage[:, 1, :]
        gate_t = stage[:, 1, ROWS:2 * ROWS]
        bias_raw = stage[:, 1, 0:D]

        class Rows:
            def __init__(self, x1, xn2, x2_hi, x2_lo, gate_t, weight_n, weight_t):
                self.x1, self.xn2, self.x2_hi, self.x2_lo = x1, xn2, x2_hi, x2_lo
                self.gate_t, self.weight_n, self.weight_t = gate_t, weight_n, weight_t

        usual = Rows(x1, xn2, x2_hi, x2_lo, gate_t, weight_n, weight_t)
        last = Rows(x1=inc[:, 1, 0:R * D].rearrange("p (r d) -> p r d", r=R), xn2=inc[:, 2, 0:R * D],
                    x2_hi=t_hi[:, 0:DH, :], x2_lo=t_lo[:, 0:DH, :], gate_t=inc[:, 3, ROWS:2 * ROWS],
                    weight_n=inc[:, 3, 0:R * E].rearrange("p (r e) -> p r e", r=R),
                    weight_t=t_hi[0:STACK, DH, :])

        def rows_of(g):
            return last if isinstance(g, int) and g == G - 1 else usual

        x_in = (stage[:, 0, :], stage[:, 1, :], x_res[:, :, :].rearrange("p r d -> p (r d)"),
                x1[:, :, :].rearrange("p r d -> p (r d)"))

        agg = [ps(f"agg{h}", [P, ROWS]) for h in range(DH)]
        tp = [ps(f"tp{k}", [P, ROWS]) for k in range(TP)]
        ffn = [ps(f"ffn{k}", [P, PAIR * D]) for k in range(FB)]
        misc = ps("misc", [P, 512])
        gate_sums = misc[0:2 * NEP, 0:ROWS]
        gate_out = misc[:, :].rearrange("p (r e) -> p r e", r=R)

        stage_landed = [sem(f"stage_landed{k}") for k in range(XS)]
        adj_landed = [sem(f"adj_landed{c}") for c in range(C)]
        x_res_landed = sem("x_res_landed")
        small_landed = sem("small_landed")
        stored = sem("stored")
        zeroed = sem("zeroed")
        consts_ready = sem("consts_ready")
        var0_ready = sem("var0_ready")
        rstd0_ready = sem("rstd0_ready")
        stats0_ready = sem("stats0_ready")
        merge0_step = sem("merge0_step")
        xn_ready = sem("xn_ready")
        xn_hi_ready = sem("xn_hi_ready")
        xn_lo_ready = sem("xn_lo_ready")
        w_hi_ready = sem("w_hi_ready")
        w_lo_ready = sem("w_lo_ready")
        counted = sem("counted")
        count_step = sem("count_step")
        root_ready = sem("root_ready")
        norm_ready = sem("norm_ready")
        scaled = sem("scaled")
        scaled_act = sem("scaled_act")
        counted_dve = sem("counted_dve")
        inc_ready = sem("inc_ready")
        transposed = sem("transposed")
        hi_ready = sem("hi_ready")
        lo_ready = sem("lo_ready")
        multiplied = sem("multiplied")
        degree_step = sem("degree_step")
        agg_out = sem("agg_out")
        agg_back = sem("agg_back")
        x1_ready = sem("x1_ready")
        stats_ready = sem("stats_ready")
        merge_step = sem("merge_step")
        var_ready = sem("var_ready")
        rstd_ready = sem("rstd_ready")
        xn2_ready = sem("xn2_ready")
        x2_turned = sem("x2_turned")
        x2_hi_ready = sem("x2_hi_ready")
        x2_lo_ready = sem("x2_lo_ready")
        gate_summed = sem("gate_summed")
        gate_t_ready = sem("gate_t_ready")
        gate_ready = sem("gate_ready")
        bias_landed = sem("bias_landed")
        bias_hi_ready = sem("bias_hi_ready")
        bias_parts_ready = sem("bias_parts_ready")
        gate_step = sem("gate_step")
        exp_ready = sem("exp_ready")
        weight_turned = sem("weight_turned")
        weight_t_ready = sem("weight_t_ready")
        experts_ready = sem("experts_ready")
        combined = sem("combined")

        def after(g, per, n):
            return g * per + n

        def x_part(t, k):
            return t[:, k * XB:(k + 1) * XB, :]

        def w_part(t, k):
            h, e = divmod(k * WE, E)
            return t[:, h, e * D:(e + WE) * D]

        def passes(fn, engine):
            for first in range(2):
                fn(first, first)
            with engine.Fori(2, G - 1) as g:
                fn(g, None)
            fn(G - 1, G - 1)

        def inc_at(j):
            first = len(INC_AFTER) if j == 0 else EARLY * R + j
            return range(first, min(EARLY * R + j + 1, R * C))

        def last_steps(n):
            steps = J - LAST_FROM
            return range(LAST_FROM + n * steps // (R * ITEMS), LAST_FROM + (n + 1) * steps // (R * ITEMS))

        def has_experts(known):
            return known is None or known >= 2

        def dve_rows(g, c):
            few = isinstance(g, int)
            return DVE_ROWS if c == C - 1 or few and g == 0 or few and g == 1 and c == C - 2 else 0

        def counts_of(g, who, upto=C):
            dve = sum(dve_rows(g, c) for c in range(upto))
            return dve if who == "dve" else upto * R - dve

        def counts_before(g, who):
            extra = 1 if who == "dve" else 0
            first = [counts_of(k, who) + extra for k in range(2)]
            if isinstance(g, int) and g < 2:
                return sum(first[:g])
            each = counts_of(2, who) + extra
            return g * each + sum(first) - 2 * each

        def chunk(c):
            return slice(c * CW, (c + 1) * CW)

        def sums(n):
            r, q = divmod(n, ITEMS)
            return r * BLOCK_SUMS + min((q + 1) * PAIR, E) + q // (ITEMS - 1)

        def scaled_by_pool(c, r):
            return min(c, EARLY) * ACT_ROWS + max(c - EARLY, 0) * R + r + 1

        block = ctx.enter_context(nc.Block())

        @block.sync
        def _(sp):
            def load_adj(g, c):
                sp.dma_start(inc[:, :, chunk(c)], adj_rows[g, :, :, chunk(c)]).then_inc(adj_landed[c], 16)

            def load_x_res(g):
                sp.dma_start(x_res[:, :, :], x_rows[g]).then_inc(x_res_landed, 16)

            def store(g, half):
                sp.wait_ge(combined, after(g, R * BLOCK_SUMS, (2 * half + 2) * BLOCK_SUMS))
                sp.dma_start(out_rows[g, :, 2 * half:2 * half + 2, :],
                             x1[:, 2 * half:2 * half + 2, :]).then_inc(stored, 16)

            def store_last(r):
                sp.wait_ge(combined, after(G - 1, R * BLOCK_SUMS, (r + 1) * BLOCK_SUMS))
                sp.dma_start(out_rows[G - 1, :, r, :], last.x1[:, r, :]).then_inc(stored, 16)

            def load_x(k):
                if k >= XS:
                    sp.wait_ge(xn_hi_ready, k - XS + 1)
                    sp.wait_ge(xn_lo_ready, k - XS + 1)
                sp.dma_start(x_in[k % XS].rearrange("p (b d) -> p b d", d=D), x_blocks[k]
                             ).then_inc(stage_landed[k % XS], 16)

            for k in range(LATE_X):
                load_x(k)
            for c in range(C):
                load_adj(0, c)
            for k in range(LATE_X, XC):
                load_x(k)
            for e in range(R):
                sp.dma_start(gate_bias[:, e, 0:E], b_gate.rearrange("(a e) -> a e", a=1).to_broadcast([P, E])
                             ).then_inc(small_landed, 16)
                sp.dma_start(gate_bias[:, e, E:NE], b_thr.rearrange("(a e) -> a e", a=1).to_broadcast([P, 1])
                             ).then_inc(small_landed, 16)
            sp.wait_ge(zeroed, 1)
            with nc.allow_non_contiguous_dma(reason="gate weights of a few bytes a row"):
                sp.dma_start(gate_raw[:, :, 0:E], w_gate.rearrange("(h p) e -> p h e", p=P)
                             ).then_inc(small_landed, 16)
                sp.dma_start(gate_raw[:, :, E:NE], w_thr.rearrange("(h p) e -> p h e", p=P)
                             ).then_inc(small_landed, 16)

            def load_weights(k):
                sp.wait_ge(xn_hi_ready, XC - XS + k + 1)
                sp.wait_ge(xn_lo_ready, XC - XS + k + 1)
                h, e = divmod(k * WE, E)
                sp.dma_start(x_in[k].rearrange("p (e f) -> p e f", e=WE),
                             w_rows[h, :, e:e + WE, :]).then_inc(stage_landed[k], 16)

            def group(g, known):
                if has_experts(known):
                    store(g - 2, 0)
                for c in range(C):
                    if known != G - 1:
                        sp.wait_ge(transposed, after(g, J, (c + 1) * CB))
                        load_adj(g + 1, c)
                    if c == 1 and has_experts(known):
                        store(g - 2, 1)
                    if known == 0 and c in WEIGHT_LOADS:
                        for k in range(WC // 2):
                            load_weights(WEIGHT_LOADS.index(c) * WC // 2 + k)
                    if known == 0 and c == C - 1:
                        sp.wait_ge(w_hi_ready, WEIGHT_LOADED)
                        sp.wait_ge(w_lo_ready, WEIGHT_LOADED)
                        load_x_res(0)
                        for n in range(BIAS_PARTS):
                            sp.dma_start(bias_raw[n * PART:n * PART + E, :], b_exp).then_inc(bias_landed, 16)
                    if c == C // 2 and known != 0:
                        sp.wait_ge(x1_ready, after(g - 1, R, R))
                        load_x_res(g)

            passes(group, sp)
            for half in range(2):
                store(G - 2, half)
            for r in range(R):
                store_last(r)
            sp.wait_ge(stored, 16 * (2 * (G - 1) + R))

        @block.gpsimd
        def _(pool):
            nc.gpsimd.memset(gate_raw[:, :, :], 0.0).then_inc(zeroed, 1)
            nc.gpsimd.memset(ident[:, :], 0.0).then_inc(zeroed, 1)
            nc.gpsimd.memset(weight_parts[:, :, :].bitcast(F32), 0.0).then_inc(zeroed, 1)
            nc.gpsimd.memset(bias_parts[:, :].bitcast(F32), 0.0).then_inc(zeroed, 1)
            nc.gpsimd.memset(minus_half[:, :], -0.5).then_inc(consts_ready, 1)
            nc.gpsimd.memset(half[:, :], 0.5).then_inc(consts_ready, 1)
            nc.gpsimd.memset(sign_bias[:, :], -2.0 ** -120).then_inc(consts_ready, 1)
            pool.wait_ge(zeroed, 4)
            nc.gpsimd.affine_select(out=ident[:, :], in_=ident[:, :], compare_op=ALU.not_equal, fill=1.0,
                                    base=0, pattern=[[-1, P]], channel_multiplier=1).then_inc(consts_ready, 1)
            pool.wait_ge(consts_ready, 4)

            def first_low(k):
                pool.wait_ge(xn_hi_ready, k + 1)
                nc.gpsimd.tensor_tensor(x_part(xn_lo, k), x_in[k % XS].rearrange("p (b d) -> p b d", d=D),
                                        x_part(xn_hi, k).bitcast(F32), ALU.subtract).then_inc(xn_lo_ready, 1)

            def first_deviation(k):
                pool.wait_ge(var0_ready, k + 1)
                nc.gpsimd.tensor_tensor(rstd0[:, k % 2, :], var0[:, k % 2, :], minus_half[:, 0:XB], ALU.pow
                                        ).then_inc(rstd0_ready, 1)

            for k in range(LATE_X):
                first_deviation(k)
                if k >= 1:
                    first_low(k - 1)
            first_low(LATE_X - 1)

            def scale_rows(g, c, r):
                if c == 0 and r == 0:
                    pool.wait_ge(norm_ready, g + 1)
                    nc.gpsimd.tensor_tensor(inc[:, r, chunk(c)], inc[:, r, chunk(c)],
                                            norm[:, r:r + 1].to_broadcast([P, CW]), ALU.mult).then_inc(scaled, 1)
                else:
                    nc.gpsimd.tensor_scalar(inc[:, r, chunk(c)], inc[:, r, chunk(c)], norm[:, r:r + 1], 1.0,
                                            ALU.mult, ALU.mult).then_inc(scaled, 1)

            def group(g, known):
                pool.wait_ge(count_step, after(g, COUNT_STEPS, 2))
                nc.gpsimd.tensor_tensor(root[:, :], count[:, :], half[:, :], ALU.pow).then_inc(root_ready, 1)
                for c in range(C):
                    for r in range(ACT_ROWS if c < EARLY else R):
                        scale_rows(g, c, r)
                    if known == 0 and c >= LATE_CHUNK:
                        k, odd = divmod(c - LATE_CHUNK, 2)
                        if odd:
                            first_low(LATE_X + k)
                        else:
                            first_deviation(LATE_X + k)
                if known == 0:
                    for k in range(LATE_X + (C - LATE_CHUNK) // 2, XC):
                        first_deviation(k)
                        first_low(k)
                if known != 0:
                    inverse_deviation(g - 1)

            def inverse_deviation(g):
                pool.wait_ge(var_ready, g + 1)
                nc.gpsimd.tensor_tensor(rstd[:, :], var[:, :], minus_half[:, 0:R], ALU.pow
                                        ).then_inc(rstd_ready, 1)

            passes(group, pool)
            inverse_deviation(G - 1)

        @block.scalar
        def _(act):
            def count_rows(g, c, r):
                if r < dve_rows(g, c):
                    return
                if r == dve_rows(g, c):
                    act.wait_ge(adj_landed[c], after(g, 16, 16))
                if not (isinstance(g, int) and g == 0 and c == 0 and r == DVE_ROWS):
                    act.wait_ge(counted, counts_before(g, "act") + counts_of(g, "act", c) + r - dve_rows(g, c))
                nc.scalar.activation(signs[:, :], inc[:, r, chunk(c)], ACT.Sign,
                                     bias=sign_bias[:, 0:1], scale=2.0 ** 100,
                                     accum_out=sign_sum[:, r, c:c + 1]).then_inc(counted, 1)

            def scale_rows(g, c):
                if c == 0:
                    act.wait_ge(norm_ready, g + 1)
                for r in range(ACT_ROWS, R):
                    nc.scalar.activation(inc[:, r, chunk(c)], inc[:, r, chunk(c)], ACT.Copy,
                                         scale=norm[:, r:r + 1]).then_inc(scaled_act, 1)

            def high(g, known, j):
                act.wait_ge(transposed, after(g, J, j + 1))
                if j >= HL or known != 0:
                    act.wait_ge(multiplied, after(g, J, j - HL + 1))
                nc.scalar.activation(t_hi[:, j % HL, :], tp[j % TP][:, :], ACT.Copy).then_inc(hi_ready, 1)

            def split_weights(k):
                act.wait_ge(stage_landed[k], 16 * (XC // XS + 1))
                nc.scalar.activation(w_part(w_hi, k), x_in[k], ACT.Copy).then_inc(w_hi_ready, 1)

            def post(g, j):
                for h in range(DH):
                    if j == TURN_AT[h] + 1:
                        act.wait_ge(x2_turned, after(g, DH, h + 1))
                        nc.scalar.activation(rows_of(g).x2_hi[:, h, :], misc[:, :], ACT.Copy).then_inc(x2_hi_ready, 1)
                if j == GATE_AT + 1:
                    act.wait_ge(gate_summed, g + 1)
                    nc.scalar.activation(rows_of(g).gate_t[0:2 * NEP, :], gate_sums, ACT.Copy).then_inc(gate_t_ready, 1)
                if j == GATE_AT + 4:
                    act.wait_ge(gate_step, after(g, GATE_STEPS, 5))
                    nc.scalar.activation(expd[:, :, :], logits[:, :, :], ACT.Exp).then_inc(exp_ready, 1)
                if j == WEIGHT_AT + 1:
                    act.wait_ge(weight_turned, g + 1)
                    nc.scalar.activation(rows_of(g).weight_t, misc[0:STACK, :], ACT.Copy).then_inc(weight_t_ready, 1)

            act.wait_ge(consts_ready, 4)

            def first_high(k):
                act.wait_ge(xn_ready, (k + 1) * XB)
                nc.scalar.activation(x_part(xn_hi, k), x_in[k % XS].rearrange("p (b d) -> p b d", d=D),
                                     ACT.Copy).then_inc(xn_hi_ready, 1)

            for k in range(max(LATE_X, C + 1)):
                if k < LATE_X:
                    first_high(k)
                if 1 <= k <= C:
                    for r in range(DVE_ROWS, R):
                        count_rows(0, k - 1, r)

            def group(g, known):
                for c in range(EARLY):
                    scale_rows(g, c)
                for j in range(AHEAD):
                    high(g, known, j)
                for j in range(J):
                    if j + AHEAD < J:
                        high(g, known, j + AHEAD)
                    n = j - COUNT_AT
                    if 0 <= n < (C - 1) * R and known != G - 1:
                        if n == 0:
                            act.wait_ge(count_step, after(g, COUNT_STEPS, 1))
                        count_rows(g + 1, n // R, n % R)
                    if known != 0:
                        post(g - 1, j)
                    if known == 1 and j == SMALL_SPLIT_AT:
                        act.wait_ge(bias_landed, 16 * BIAS_PARTS)
                        for n in range(BIAS_PARTS):
                            part = slice(n * PART, n * PART + E)
                            nc.scalar.activation(bias_parts[part, :], bias_raw[part, :], ACT.Copy
                                                 ).then_inc(bias_hi_ready, 1)
                        act.wait_ge(small_landed, 16 * SMALL_LOADS)
                        nc.scalar.activation(gate_w[:, :, 0:NEP], gate_raw[:, :, :], ACT.Copy).then_inc(w_hi_ready, 1)
                    if known == 0 and j - SPLIT_STEP in LATE_AT:
                        first_high(LATE_X + LATE_AT.index(j - SPLIT_STEP))
                    if known == 0 and j in WEIGHT_SPLITS:
                        split_weights(WEIGHT_SPLITS.index(j))
                if known != G - 1:
                    for n in range(J - COUNT_AT, (C - 1) * R):
                        count_rows(g + 1, n // R, n % R)
                act.wait_ge(multiplied, after(g, J, J))
                if known == 0:
                    act.wait_ge(w_lo_ready, WC)
                for h in range(DH):
                    if known != 0 and h == 0:
                        act.wait_ge(agg_back, after(g - 1, 2, 2))
                    nc.scalar.activation(agg_t[:, h * ROWS:(h + 1) * ROWS], agg[h][:, :], ACT.Copy
                                         ).then_inc(agg_out, 1)
                if known != G - 1:
                    for r in range(R):
                        count_rows(g + 1, C - 1, r)

            passes(group, act)
            for j in range(LAST_FROM, J):
                post(G - 1, j)

        @block.vector
        def _(dve):
            def low(g, j):
                dve.wait_ge(hi_ready, after(g, J, j + 1))
                nc.vector.tensor_tensor(t_lo[:, j % HL, :], tp[j % TP][:, :], t_hi[:, j % HL, :].bitcast(F32),
                                        ALU.subtract).then_inc(lo_ready, 1)

            def row_counts(g):
                dve.wait_ge(counted, counts_before(g, "act") + counts_of(g, "act"))
                dve.wait_ge(counted_dve, counts_before(g, "dve") + counts_of(g, "dve") + 1)
                nc.vector.tensor_reduce(sign_row[:, :], sign_sum[:, :, :], AX.X, ALU.add).then_inc(count_step, 1)
                dve.wait_ge(count_step, after(g, COUNT_STEPS, 1))
                nc.vector.tensor_scalar(count[:, :], sign_row[:, :], float(N), 0.5, ALU.add, ALU.mult
                                        ).then_inc(count_step, 1)

            def norms(g):
                dve.wait_ge(root_ready, g + 1)
                nc.vector.tensor_scalar(norm[:, :], root[:, :], NORM_EPS, None, ALU.max).then_inc(norm_ready, 1)

            def count_chunk(g, c):
                dve.wait_ge(adj_landed[c], after(g, 16, 16))
                for r in range(dve_rows(g, c)):
                    n = counts_of(g, "dve", c) + r
                    if n >= HL:
                        dve.wait_ge(counted_dve, n - HL + 1)
                    nc.vector.scalar_tensor_tensor(t_lo[:, n % HL, :], inc[:, r, chunk(c)], 0.0,
                                                   minus_half[:, 0:1].to_broadcast([P, CW]), ALU.is_gt, ALU.add,
                                                   accum_out=sign_sum[:, r, c:c + 1]).then_inc(counted_dve, 1)

            def double(g, chunks):
                dve.wait_ge(counted_dve, counts_before(g, "dve") + counts_of(g, "dve"))
                part = sign_sum[:, 0:DVE_ROWS, chunks]
                nc.vector.tensor_scalar(part, part, 2.0, None, ALU.mult).then_inc(counted_dve, 1)

            def make_inc(g, c, r):
                if c < EARLY and r >= ACT_ROWS:
                    dve.wait_ge(scaled_act, after(g, EARLY * (R - ACT_ROWS), c * (R - ACT_ROWS) + r - ACT_ROWS + 1))
                else:
                    dve.wait_ge(scaled, after(g, scaled_by_pool(C - 1, R - 1), scaled_by_pool(c, r)))
                part = inc[:, r, chunk(c)]
                nc.vector.scalar_tensor_tensor(part, part, 0.0, part, ALU.is_gt, ALU.add,
                                               accum_out=degree_part[:, r, c:c + 1]).then_inc(inc_ready, 1)

            def degrees(g):
                dve.wait_ge(inc_ready, after(g, R * C, R * C))
                nc.vector.tensor_reduce(degree[:, :], degree_part[:, :, :], AX.X, ALU.add).then_inc(degree_step, 1)
                dve.wait_ge(degree_step, after(g, 2, 1))
                nc.vector.reciprocal(inv_degree[:, :], degree[:, :]).then_inc(degree_step, 1)

            def merge(st, mean_out, var_out, tmp, step, done, var_done):
                m0, q0, m1, q1 = (st[:, :, n] for n in (1, 2, 4, 5))
                nc.vector.tensor_tensor(tmp[:, 0, :], m0, m1, ALU.add).then_inc(done, 1)
                nc.vector.tensor_tensor(tmp[:, 1, :], m0, m1, ALU.subtract).then_inc(done, 1)
                nc.vector.tensor_tensor(tmp[:, 2, :], q0, q1, ALU.add).then_inc(done, 1)
                step(1)
                nc.vector.tensor_scalar(mean_out, tmp[:, 0, :], 0.5, None, ALU.mult)
                step(2)
                nc.vector.scalar_tensor_tensor(tmp[:, 1, :], tmp[:, 1, :], 0.25, tmp[:, 1, :], ALU.mult, ALU.mult
                                               ).then_inc(done, 1)
                step(3)
                nc.vector.tensor_scalar(tmp[:, 2, :], tmp[:, 2, :], 1.0 / D, LN_EPS, ALU.mult, ALU.add
                                        ).then_inc(done, 1)
                step(5)
                nc.vector.tensor_tensor(var_out, tmp[:, 1, :], tmp[:, 2, :], ALU.add).then_inc(var_done, 1)

            def add_aggregate(g, r):
                if r % 2 == 0:
                    dve.wait_ge(agg_back, after(g, 2, r // 2 + 1))
                if r == 0:
                    dve.wait_ge(x_res_landed, after(g, 16, 16))
                    if not (isinstance(g, int) and g in (0, G - 1)):
                        dve.wait_ge(stored, after(g, 32, 0))
                    dve.wait_ge(degree_step, after(g, 2, 2))
                nc.vector.scalar_tensor_tensor(rows_of(g).x1[:, r, :], misc[:, (r % 2) * D:(r % 2 + 1) * D],
                                               inv_degree[:, r:r + 1], x_res[:, r, :], ALU.mult, ALU.add
                                               ).then_inc(x1_ready, 1)

            def statistics(g, half):
                for r in (2 * half, 2 * half + 1):
                    dve.wait_ge(x1_ready, after(g, R, r + 1))
                    nc.vector.bn_stats(stats[:, r, :], rows_of(g).x1[:, r, :]).then_inc(stats_ready, 1)

            def merge_statistics(g):
                dve.wait_ge(stats_ready, after(g, R, R))
                merge(stats, mean[:, :], var[:, :], parts, lambda n: dve.wait_ge(merge_step, after(g, 5, n)),
                      merge_step, var_ready)

            def normalise(g, half):
                if half == 0:
                    dve.wait_ge(rstd_ready, g + 1)
                for r in (2 * half, 2 * half + 1):
                    nc.vector.tensor_scalar(rows_of(g).xn2[:, r * D:(r + 1) * D], rows_of(g).x1[:, r, :],
                                            mean[:, r:r + 1], rstd[:, r:r + 1], ALU.subtract, ALU.mult
                                            ).then_inc(xn2_ready, 1)

            def turn_low(g, h):
                dve.wait_ge(x2_hi_ready, after(g, DH, h + 1))
                rows = rows_of(g)
                nc.vector.tensor_tensor(rows.x2_lo[:, h, :], misc[:, :], rows.x2_hi[:, h, :].bitcast(F32), ALU.subtract
                                        ).then_inc(x2_lo_ready, 1)

            wide = lambda a: a[:, :].unsqueeze(2).to_broadcast([P, R, E])

            def gate_exponents(g):
                def step(n):
                    dve.wait_ge(gate_step, after(g, GATE_STEPS, n))

                dve.wait_ge(gate_ready, g + 1)
                nc.vector.tensor_tensor(logits[:, :, :], gate_out[:, :, 0:NE], gate_bias[:, :, :], ALU.add
                                        ).then_inc(gate_step, 1)
                step(1)
                nc.vector.tensor_tensor(logits[:, :, :], gate_out[:, :, NEP:NEP + NE], logits[:, :, :], ALU.add
                                        ).then_inc(gate_step, 1)
                step(2)
                nc.vector.tensor_reduce(top[:, :], logits[:, :, 0:E], AX.X, ALU.max).then_inc(gate_step, 1)
                nc.vector.tensor_scalar(logits[:, :, E:NE], logits[:, :, E:NE], -1.0, None, ALU.mult
                                        ).then_inc(gate_step, 1)
                step(3)
                nc.vector.tensor_tensor(logits[:, :, 0:E], logits[:, :, 0:E], wide(top), ALU.subtract
                                        ).then_inc(gate_step, 1)

            def gate_weights(g):
                def step(n):
                    dve.wait_ge(gate_step, after(g, GATE_STEPS, n))

                dve.wait_ge(exp_ready, g + 1)
                nc.vector.tensor_reduce(total[:, :], expd[:, :, 0:E], AX.X, ALU.add).then_inc(gate_step, 1)
                nc.vector.tensor_scalar(thr[:, :], expd[:, :, E], 1.0, None, ALU.add).then_inc(gate_step, 1)
                step(6)
                nc.vector.reciprocal(inv_total[:, :], total[:, :]).then_inc(gate_step, 1)
                step(7)
                nc.vector.reciprocal(thr[:, :], thr[:, :]).then_inc(gate_step, 1)
                step(8)
                nc.vector.tensor_tensor(weight[:, :, :], expd[:, :, 0:E], wide(inv_total), ALU.mult
                                        ).then_inc(gate_step, 1)
                step(10)
                nc.vector.scalar_tensor_tensor(weight[:, :, :], wide(thr), -MAX_THRESHOLD, weight[:, :, :],
                                               ALU.mult, ALU.add).then_inc(gate_step, 1)
                step(11)
                nc.vector.scalar_tensor_tensor(weight[:, :, :], weight[:, :, :], 0.0, weight[:, :, :],
                                               ALU.is_ge, ALU.mult).then_inc(gate_step, 1)
                step(12)
                nc.vector.tensor_reduce(wsum[:, :], weight[:, :, :], AX.X, ALU.add).then_inc(gate_step, 1)
                step(13)
                nc.vector.scalar_tensor_tensor(wsum[:, :], wsum[:, :], 0.0, wsum[:, :], ALU.is_equal, ALU.add
                                               ).then_inc(gate_step, 1)
                step(14)
                nc.vector.reciprocal(inv_wsum[:, :], wsum[:, :]).then_inc(gate_step, 1)
                step(15)
                exact = rows_of(g).weight_n
                nc.vector.tensor_tensor(exact, weight[:, :, :], wide(inv_wsum), ALU.mult).then_inc(gate_step, 1)
                step(16)
                for n in (1, 2):
                    nc.vector.tensor_scalar(weight_parts[:, :, n * PART:n * PART + E], exact, 1.0, None, ALU.mult
                                            ).then_inc(gate_step, 1)
                step(17)
                nc.vector.tensor_tensor(weight_parts[:, :, 0:E], exact, weight_parts[:, :, PART:PART + E].bitcast(F32),
                                        ALU.subtract).then_inc(gate_step, 1)

            def combine(g, n):
                r, q = divmod(n, ITEMS)
                rows = rows_of(g)
                acc = rows.x1
                dve.wait_ge(experts_ready, after(g, R * ITEMS, n + 1))
                bank = ffn[n % FB]
                if q < ITEMS - 1:
                    for i in range(PAIR):
                        e = q * PAIR + i
                        if e > 0:
                            dve.wait_ge(combined, after(g, R * BLOCK_SUMS, r * BLOCK_SUMS + e))
                        nc.vector.scalar_tensor_tensor(acc[:, r, :], bank[:, i * D:(i + 1) * D],
                                                       rows.weight_n[:, r, e:e + 1], acc[:, r, :],
                                                       ALU.mult, ALU.add).then_inc(combined, 1)
                else:
                    dve.wait_ge(combined, after(g, R * BLOCK_SUMS, r * BLOCK_SUMS + E))
                    nc.vector.tensor_tensor(acc[:, r, :], bank[:, 0:D], acc[:, r, :], ALU.add
                                            ).then_inc(combined, 1)

            def post(g, j):
                for n in range(2):
                    if j == BACK_AT[n] + 1:
                        add_aggregate(g, 2 * n)
                        add_aggregate(g, 2 * n + 1)
                    if j == STAT_AT[n]:
                        statistics(g, n)
                    if j == NORMAL_AT[n]:
                        normalise(g, n)
                if j == MERGE_AT:
                    merge_statistics(g)
                for h in range(DH):
                    if j == TURN_AT[h] + 1:
                        turn_low(g, h)
                if j == GATE_AT + 3:
                    gate_exponents(g)
                if j == GATE_AT + 5:
                    gate_weights(g)

            dve.wait_ge(consts_ready, 4)

            def first_statistics(k, part):
                xs = x_in[k % XS].rearrange("p (b d) -> p b d", d=D)
                if part == 0:
                    dve.wait_ge(stage_landed[k % XS], 16 * (k // XS + 1))
                for b in range(part * XB // 2, (part + 1) * XB // 2):
                    nc.vector.bn_stats(stats0[:, b, :], xs[:, b, :]).then_inc(stats0_ready, 1)

            def first_merge(k):
                dve.wait_ge(stats0_ready, (k + 1) * XB)
                merge(stats0, mean0[:, k % 2, :], var0[:, k % 2, :], parts0,
                      lambda n: dve.wait_ge(merge0_step, 5 * k + n), merge0_step, var0_ready)

            def first_normalise(k, part):
                xs = x_in[k % XS].rearrange("p (b d) -> p b d", d=D)
                dve.wait_ge(rstd0_ready, k + 1)
                for b in range(part * XB // 2, (part + 1) * XB // 2):
                    nc.vector.tensor_scalar(xs[:, b, :], xs[:, b, :], mean0[:, k % 2, b:b + 1],
                                            rstd0[:, k % 2, b:b + 1], ALU.subtract, ALU.mult
                                            ).then_inc(xn_ready, 1)

            for k in range(LATE_X + 1):
                if k < LATE_X:
                    for part in range(2):
                        first_statistics(k, part)
                    first_merge(k)
                if k >= 1:
                    for part in range(2):
                        first_normalise(k - 1, part)
            for c in range(C):
                count_chunk(0, c)
            double(0, slice(0, C))

            def late_norm(j):
                for i, first in enumerate(LATE_AT):
                    for part in range(2):
                        if j == first + part:
                            first_statistics(LATE_X + i, part)
                    if j == first + MERGE_STEP:
                        first_merge(LATE_X + i)
                    for part in range(2):
                        if j == first + NORMAL_STEPS[part]:
                            first_normalise(LATE_X + i, part)

            def group(g, known):
                for n in range(FIRST_ITEMS):
                    if has_experts(known):
                        combine(g - 2, n)
                    if n == COUNT_AFTER and known != 0:
                        dve.wait_ge(multiplied, after(g - 1, J, J))
                        for c in (C - 2, C - 1) if known == 1 else (C - 1,):
                            count_chunk(g, c)
                        double(g, slice(C - 2 if known == 1 else C - 1, C))
                    if n == NORMS_AFTER:
                        row_counts(g)
                    if n == NORMS_AFTER + 1:
                        norms(g)
                    for k in range(len(INC_AFTER)):
                        if n == INC_AFTER[k]:
                            make_inc(g, k // R, k % R)
                    if n in TURN_AFTER:
                        low(g, TURN_AFTER.index(n))
                for j in range(J):
                    if j + AHEAD < J:
                        low(g, j + AHEAD)
                    if known == 1 and j == SMALL_SPLIT_AT:
                        dve.wait_ge(bias_hi_ready, BIAS_PARTS)
                        mid = slice(PART, PART + E)
                        nc.vector.tensor_tensor(bias_parts[mid, :], bias_raw[mid, :], bias_parts[mid, :].bitcast(F32),
                                                ALU.subtract).then_inc(bias_parts_ready, 1)
                        dve.wait_ge(w_hi_ready, WC + 1)
                        nc.vector.tensor_tensor(gate_w[:, :, NEP:2 * NEP], gate_raw[:, :, :],
                                                gate_w[:, :, 0:NEP].bitcast(F32), ALU.subtract).then_inc(w_lo_ready, 1)
                    for n in inc_at(j):
                        make_inc(g, n // R, n % R)
                    if known == 0:
                        late_norm(j)
                    if has_experts(known) and FIRST_ITEMS + j < R * ITEMS:
                        combine(g - 2, FIRST_ITEMS + j)
                    if known != 0:
                        post(g - 1, j)
                    if known == 0 and j in WEIGHT_SPLITS:
                        k = WEIGHT_SPLITS.index(j)
                        dve.wait_ge(w_hi_ready, k + 1)
                        nc.vector.tensor_tensor(w_part(w_lo, k), x_in[k], w_part(w_hi, k).bitcast(F32),
                                                ALU.subtract).then_inc(w_lo_ready, 1)
                degrees(g)

            passes(group, dve)
            for n in range(R * ITEMS):
                for j in last_steps(n):
                    post(G - 1, j)
                combine(G - 2, n)
            for n in range(R * ITEMS):
                combine(G - 1, n)

        @block.tensor
        def _(pe):
            def turn(g, j):
                if j % CB == 0:
                    pe.wait_ge(inc_ready, after(g, R * C, (j // CB + 1) * R))
                if j >= TP:
                    pe.wait_ge(lo_ready, after(g, J, j - TP + 1))
                for r in range(R):
                    mm = nc.tensor.transpose(tp[j % TP][:, r * P:(r + 1) * P], inc[:, r, j * P:(j + 1) * P],
                                             ident[:, :])
                mm.then_inc(transposed, 1)

            def multiply(g, known, j):
                pe.wait_ge(lo_ready, after(g, J, j + 1))
                if j == 0 and known != 0:
                    pe.wait_ge(agg_out, after(g - 1, DH, DH))
                if known == 0 and (j == 0 or j >= LATE_X * XB and j % XB == 0):
                    pe.wait_ge(xn_lo_ready, max(j // XB + 1, LATE_X))
                for h in range(DH):
                    f = slice(h * P, (h + 1) * P)
                    parts = ((xn_lo, t_hi), (xn_hi, t_lo), (xn_hi, t_hi))
                    for n, (a, b) in enumerate(parts):
                        mm = nc.tensor.matmul(agg[h][:, :], a[:, j, f], b[:, j % HL, :],
                                              start=(j == 0 and n == 0), stop=(j == J - 1 and n == len(parts) - 1))
                mm.then_inc(multiplied, 1)

            def experts(g, n):
                r, q = divmod(n, ITEMS)
                cols_r = slice(r * P, (r + 1) * P)
                rows = rows_of(g)
                if n >= FB:
                    pe.wait_ge(combined, after(g, R * BLOCK_SUMS, sums(n - FB)))
                elif rows is last:
                    pe.wait_ge(combined, after(g - 1, R * BLOCK_SUMS, sums(R * ITEMS - FB + (n - R * ITEMS) % FB)))
                bank = ffn[n % FB]
                if q < ITEMS - 1:
                    cols = slice(q * PAIR * D, (q + 1) * PAIR * D)
                    parts = [(a, b, h) for h in range(DH)
                             for a, b in ((rows.x2_lo, w_hi), (rows.x2_hi, w_lo), (rows.x2_hi, w_hi))]
                    for i, (a, b, h) in enumerate(parts):
                        mm = nc.tensor.matmul(bank[:, :], a[:, h, cols_r], b[:, h, cols],
                                              start=(i == 0), stop=(i == len(parts) - 1))
                else:
                    if r == 0:
                        pe.wait_ge(weight_t_ready, g + 1)
                    mm = nc.tensor.matmul(bank[:, 0:D], rows.weight_t[:, cols_r], bias_parts[:, :],
                                          start=True, stop=True)
                mm.then_inc(experts_ready, 1)

            def post(g, j):
                for n in range(2):
                    if j == BACK_AT[n]:
                        pe.wait_ge(agg_out, after(g, DH, DH))
                        if n == 1:
                            pe.wait_ge(x1_ready, after(g, R, 2))
                        for r in (2 * n, 2 * n + 1):
                            for h in range(DH):
                                col = (r % 2) * D + h * P
                                mm = nc.tensor.transpose(misc[:, col:col + P],
                                                         agg_t[:, h * ROWS + r * P:h * ROWS + (r + 1) * P], ident[:, :])
                        mm.then_inc(agg_back, 1)
                for h in range(DH):
                    if j == TURN_AT[h]:
                        if h == 0:
                            pe.wait_ge(xn2_ready, after(g, R, R))
                        else:
                            pe.wait_ge(x2_lo_ready, after(g, DH, h))
                        for r in range(R):
                            mm = nc.tensor.transpose(misc[:, r * P:(r + 1) * P],
                                                     rows_of(g).xn2[:, r * D + h * P:r * D + (h + 1) * P], ident[:, :])
                        mm.then_inc(x2_turned, 1)
                if j == GATE_AT:
                    pe.wait_ge(x2_lo_ready, after(g, DH, DH))
                    parts = [(part, h) for h in range(DH) for part in (rows_of(g).x2_lo, rows_of(g).x2_hi)]
                    for i, (part, h) in enumerate(parts):
                        mm = nc.tensor.matmul(gate_sums, gate_w[:, h, :], part[:, h, :],
                                              start=(i == 0), stop=(i == len(parts) - 1))
                    mm.then_inc(gate_summed, 1)
                if j == GATE_AT + 2:
                    pe.wait_ge(gate_t_ready, g + 1)
                    for r in range(R):
                        mm = nc.tensor.transpose(gate_out[:, r, :], rows_of(g).gate_t[:, r * P:(r + 1) * P],
                                                 ident[:, :])
                    mm.then_inc(gate_ready, 1)
                if j == WEIGHT_AT:
                    pe.wait_ge(gate_step, after(g, GATE_STEPS, GATE_STEPS))
                    for r in range(R):
                        mm = nc.tensor.transpose(misc[0:STACK, r * P:(r + 1) * P],
                                                 weight_parts[:, r, :].bitcast(F32), ident[:, :])
                    mm.then_inc(weight_turned, 1)

            pe.wait_ge(consts_ready, 4)

            def group(g, known):
                for n in range(FIRST_ITEMS):
                    if has_experts(known):
                        experts(g - 2, n)
                    if n in TURN_AFTER:
                        turn(g, TURN_AFTER.index(n))
                for j in range(J):
                    if j + AHEAD < J:
                        turn(g, j + AHEAD)
                    multiply(g, known, j)
                    if has_experts(known) and FIRST_ITEMS + j < R * ITEMS:
                        experts(g - 2, FIRST_ITEMS + j)
                    if known == 1 and j == BACK_AT[0]:
                        pe.wait_ge(w_lo_ready, WC + 1)
                        pe.wait_ge(bias_parts_ready, 1)
                    if known != 0:
                        post(g - 1, j)

            passes(group, pe)
            for n in range(R * ITEMS):
                experts(G - 2, n)
                for j in last_steps(n):
                    post(G - 1, j)
            for n in range(R * ITEMS):
                experts(G - 1, n)


_INS = ['x', 'adj', 'L0_ffn_W_gate', 'L0_ffn_b_gate', 'L0_ffn_W_thr', 'L0_ffn_b_thr', 'L0_ffn_W_exp', 'L0_ffn_b_exp']
_OUTS = [((4096, 256), 'float32')]


def kernel(**inputs):
    import numpy as _np
    import concourse.bacc as _bacc
    from concourse import mybir as _mybir
    from concourse.bass_utils import run_bass_kernel_spmd as _run

    nc = _bacc.Bacc("TRN2", target_bir_lowering=False, num_devices=1)
    arrays, args = {}, []
    for name in _INS:
        a = _np.ascontiguousarray(inputs[name])
        arrays[f"in_{name}_dram"] = a
        args.append(nc.dram_tensor(f"in_{name}_dram", a.shape, _mybir.dt.from_np(a.dtype), kind="ExternalInput").ap())
    for i, (shape, dtype) in enumerate(_OUTS):
        dt = _mybir.dt.from_np(_np.dtype(dtype))
        args.append(nc.dram_tensor(f"out_{i}_dram", shape, dt, kind="ExternalOutput").ap())
    program(nc, *args)
    r = _run(nc, [arrays], core_ids=[0])
    return r.results[0]["out_0_dram"]
```
